# Optimizing a Trainium2 kernel written in Bass

```python
import numpy as np
import jax
import jax.numpy as jnp

def _softmax(x, axis=-1):
    return jax.nn.softmax(x, axis=axis)

def _gelu(x):
    return jax.nn.gelu(x, approximate=True)

def _silu(x):
    return jax.nn.silu(x)

def _sigmoid(x):
    return jax.nn.sigmoid(x)

def _layernorm(x, axis=-1, eps=1e-05):
    m = jnp.mean(x, axis=axis, keepdims=True)
    v = jnp.var(x, axis=axis, keepdims=True)
    return (x - m) / jnp.sqrt(v + eps)

def _scatter_add(tgt, idx, src, axis=0):
    return tgt.at[idx].add(src)

def _segment_sum(src, seg, n):
    return jax.ops.segment_sum(src, seg, n)
kernel_name = 'mk_adaln_d1_jaxref_r8_6d8f80'

def setup_inputs(seed: int=0):
    np.random.seed(seed)
    _w = jnp.asarray

    def _L0_attn_setup():
        import jax, jax.numpy as jnp
        import numpy as np
        HIDDEN = 128
        MEM = 32
        DECAY = 0.99

        def _reference_tuple_inner(x, Wq, Wk, Wv, Wo, gate, M0):
            b = x.shape[0]
            q = jnp.einsum('bsh,mh->bsm', x, Wq)
            k = jnp.einsum('bsh,mh->bsm', x, Wk)
            v = jnp.einsum('bsh,mh->bsm', x, Wv)
            qT = jnp.swapaxes(q, 0, 1)
            kT = jnp.swapaxes(k, 0, 1)
            vT = jnp.swapaxes(v, 0, 1)

            def step(M, qkv):
                q_t, k_t, v_t = qkv
                r_t = q_t @ M.T
                outer = v_t.T @ k_t / b
                M_new = DECAY * M + outer
                return (M_new, r_t)
            _, rT = jax.lax.scan(step, M0, (qT, kT, vT))
            retrieved = jnp.swapaxes(rT, 0, 1)
            output = jnp.einsum('bsm,hm->bsh', retrieved, Wo)
            gate_value = jax.nn.sigmoid(gate)
            return (output * gate_value, gate_value)
        key = jax.random.key(seed)
        ks = jax.random.split(key, 6)
        x = jax.random.normal(ks[0], (4, 512, HIDDEN), dtype=jnp.float32)
        scale = 0.02
        Wq = jax.random.normal(ks[1], (MEM, HIDDEN), dtype=jnp.float32) * scale
        Wk = jax.random.normal(ks[2], (MEM, HIDDEN), dtype=jnp.float32) * scale
        Wv = jax.random.normal(ks[3], (MEM, HIDDEN), dtype=jnp.float32) * scale
        Wo = jax.random.normal(ks[4], (HIDDEN, MEM), dtype=jnp.float32) * scale
        gate = jnp.zeros((1,), dtype=jnp.float32)
        M0 = jnp.zeros((MEM, MEM), dtype=jnp.float32)
        return {'x': x, 'Wq': Wq, 'Wk': Wk, 'Wv': Wv, 'Wo': Wo, 'gate': gate, 'M0': M0}
    _L0_attn_in = _L0_attn_setup()

    def _L0_ffn_setup():
        import jax, jax.numpy as jnp
        import numpy as np
        D_MODEL = 128
        D_FF = 512
        NUM_EXPERTS = 8
        TOP_K = 2
        key = jax.random.key(seed)
        ks = jax.random.split(key, 8)
        s_in = 1.0 / np.sqrt(D_MODEL)
        s_ff = 1.0 / np.sqrt(D_FF)
        x = jax.random.normal(ks[0], (2, 256, D_MODEL), dtype=jnp.float32)
        Wg = jax.random.uniform(ks[1], (D_MODEL, NUM_EXPERTS), minval=-s_in, maxval=s_in, dtype=jnp.float32)
        bg = jax.random.uniform(ks[2], (NUM_EXPERTS,), minval=-s_in, maxval=s_in, dtype=jnp.float32)
        W1 = jax.random.uniform(ks[3], (NUM_EXPERTS, D_MODEL, D_FF), minval=-s_in, maxval=s_in, dtype=jnp.float32)
        b1 = jax.random.uniform(ks[4], (NUM_EXPERTS, D_FF), minval=-s_in, maxval=s_in, dtype=jnp.float32)
        W2 = jax.random.uniform(ks[5], (NUM_EXPERTS, D_FF, D_MODEL), minval=-s_ff, maxval=s_ff, dtype=jnp.float32)
        b2 = jax.random.uniform(ks[6], (NUM_EXPERTS, D_MODEL), minval=-s_ff, maxval=s_ff, dtype=jnp.float32)
        return {'x': x, 'Wg': Wg, 'bg': bg, 'W1': W1, 'b1': b1, 'W2': W2, 'b2': b2}
    _L0_ffn_in = _L0_ffn_setup()
    _L0_c = _w((lambda *s: np.random.randn(*s).astype(np.float32) * 0.05)(32, 128))
    _L0_wmod = _w((lambda *s: np.random.randn(*s).astype(np.float32) * 0.05)(128, 6 * 128) * 128 ** (-0.5))
    _d = {'L0_attn_x': _L0_attn_in['x'], 'L0_attn_Wq': _L0_attn_in['Wq'], 'L0_attn_Wk': _L0_attn_in['Wk'], 'L0_attn_Wv': _L0_attn_in['Wv'], 'L0_attn_Wo': _L0_attn_in['Wo'], 'L0_attn_gate': _L0_attn_in['gate'], 'L0_attn_M0': _L0_attn_in['M0'], 'L0_ffn_Wg': _L0_ffn_in['Wg'], 'L0_ffn_bg': _L0_ffn_in['bg'], 'L0_ffn_W1': _L0_ffn_in['W1'], 'L0_ffn_b1': _L0_ffn_in['b1'], 'L0_ffn_W2': _L0_ffn_in['W2'], 'L0_ffn_b2': _L0_ffn_in['b2'], 'L0_c': _L0_c, 'L0_wmod': _L0_wmod}
    _x0 = _d['L0_attn_x']
    _d['L0_attn_x'] = jax.random.normal(jax.random.fold_in(jax.random.key(seed), 1), (32, 256, 128), dtype=_x0.dtype)
    del _x0
    return _d

def reference(L0_attn_x, L0_attn_Wq, L0_attn_Wk, L0_attn_Wv, L0_attn_Wo, L0_attn_gate, L0_attn_M0, L0_ffn_Wg, L0_ffn_bg, L0_ffn_W1, L0_ffn_b1, L0_ffn_W2, L0_ffn_b2, L0_c, L0_wmod):

    def _L0_attn_ref(x, Wq, Wk, Wv, Wo, gate, M0):
        import jax, jax.numpy as jnp
        import numpy as np
        HIDDEN = 128
        MEM = 32
        DECAY = 0.99

        def _reference_tuple_inner(x, Wq, Wk, Wv, Wo, gate, M0):
            b = x.shape[0]
            q = jnp.einsum('bsh,mh->bsm', x, Wq)
            k = jnp.einsum('bsh,mh->bsm', x, Wk)
            v = jnp.einsum('bsh,mh->bsm', x, Wv)
            qT = jnp.swapaxes(q, 0, 1)
            kT = jnp.swapaxes(k, 0, 1)
            vT = jnp.swapaxes(v, 0, 1)

            def step(M, qkv):
                q_t, k_t, v_t = qkv
                r_t = q_t @ M.T
                outer = v_t.T @ k_t / b
                M_new = DECAY * M + outer
                return (M_new, r_t)
            _, rT = jax.lax.scan(step, M0, (qT, kT, vT))
            retrieved = jnp.swapaxes(rT, 0, 1)
            output = jnp.einsum('bsm,hm->bsh', retrieved, Wo)
            gate_value = jax.nn.sigmoid(gate)
            return (output * gate_value, gate_value)
        return _reference_tuple_inner(x, Wq, Wk, Wv, Wo, gate, M0)[0]

    def _L0_ffn_ref(x, Wg, bg, W1, b1, W2, b2):
        import jax, jax.numpy as jnp
        import numpy as np
        D_MODEL = 128
        D_FF = 512
        NUM_EXPERTS = 8
        TOP_K = 2
        gate_logits = jnp.einsum('bsd,de->bse', x, Wg) + bg
        gate_probs = jax.nn.softmax(gate_logits, axis=-1)
        topk_probs, topk_idx = jax.lax.top_k(gate_probs, TOP_K)
        topk_probs = topk_probs / jnp.sum(topk_probs, axis=-1, keepdims=True)
        onehot = jax.nn.one_hot(topk_idx, NUM_EXPERTS, dtype=x.dtype)
        weights = jnp.einsum('bske,bsk->bse', onehot, topk_probs)
        h = jnp.einsum('bsd,edf->bsef', x, W1) + b1
        h = jax.nn.gelu(h, approximate=False)
        y = jnp.einsum('bsef,efd->bsed', h, W2) + b2
        return jnp.einsum('bsed,bse->bsd', y, weights)
    x = L0_attn_x
    mod = (_silu(L0_c) @ L0_wmod).reshape(L0_c.shape[0], 6, 1, -1)
    sa, ca, ga, sb, cb, gb = (mod[:, 0], mod[:, 1], mod[:, 2], mod[:, 3], mod[:, 4], mod[:, 5])
    ga = (2 * (ga >= 0) - 1) * jnp.maximum(jnp.abs(ga), 0.25)
    gb = (2 * (gb >= 0) - 1) * jnp.maximum(jnp.abs(gb), 0.25)
    h = _layernorm(x, axis=-1) * (1 + ca) + sa
    x = x + ga * _L0_attn_ref(h, L0_attn_Wq, L0_attn_Wk, L0_attn_Wv, L0_attn_Wo, L0_attn_gate, L0_attn_M0)
    h = _layernorm(x, axis=-1) * (1 + cb) + sb
    x = x + gb * _L0_ffn_ref(h, L0_ffn_Wg, L0_ffn_bg, L0_ffn_W1, L0_ffn_b1, L0_ffn_W2, L0_ffn_b2)
    return x

_drawn_inputs = setup_inputs


def setup_inputs(seed=0):
    import zlib

    import numpy as np

    out = dict(_drawn_inputs(seed))
    spreads = {'L0_attn_M0': (0.0, 2.0)}
    factors = {'L0_attn_Wq': 8.0,
     'L0_attn_Wk': 8.0,
     'L0_attn_Wv': 8.0,
     'L0_attn_Wo': 8.0,
     'L0_ffn_bg': 53.552,
     'L0_ffn_b1': 64.0,
     'L0_ffn_b2': 200.0,
     'L0_ffn_Wg': 8.0,
     'L0_ffn_W1': 8.0,
     'L0_ffn_W2': 8.0}
    for name, (base, spread) in spreads.items():
        noise = np.random.default_rng([zlib.crc32(name.encode()), seed]).standard_normal(out[name].shape)
        drawn = base * np.exp(spread * noise) if base else spread * noise
        out[name] = jnp.asarray(drawn.astype(out[name].dtype))
    for name, factor in factors.items():
        out[name] = (out[name] * factor).astype(out[name].dtype)
    return out
```

```python
from contextlib import ExitStack

import numpy as np
import concourse.bass as bass
from concourse import mybir

F32 = mybir.dt.float32
F32R = mybir.dt.float32r
BF16 = mybir.dt.bfloat16
I32 = mybir.dt.int32
U32 = mybir.dt.uint32
ALU = mybir.AluOpType
ACT = mybir.ActivationFunctionType
AX_X = mybir.AxisListType.X

P = 128
NB = 32
NT = 256
D = 128
MEM = 32
NE = 8
DFF = 512
FB = DFF // P
TI = P // NB
NCH = NT // TI
BC = 4
NG = NCH // BC
NTOK = NB * NT
REG = NTOK + P
ROWW = 132
PAD_ROW = NE * REG
NROWS = PAD_ROW + P
NTILE = 2 * NTOK // P + NE
HALF = NE * DFF // 2
SLOTS = 4
SKIP = 1 << 20
DECAY = 0.99
EPS = 1e-5


def shape_constants():
    p = np.arange(P)
    ti = p // NB
    before = ti[:, None] < ti[None, :]
    mask = np.where(before, DECAY ** (-1.0 - ti[:, None]) / NB, 0.0).astype(np.float32)
    mask = np.broadcast_to(mask, (P, P))
    qdecay = np.tile((DECAY ** ti)[None, None, :], (MEM, BC, 1)).reshape(MEM, BC * P).astype(np.float32)
    kscale = (DECAY ** (TI - 1.0 - ti) / NB).astype(np.float32)[:, None]
    ident = np.eye(P, dtype=np.float32)
    tri = (p[:, None] < p[None, :]).astype(np.float32)
    eye8 = np.broadcast_to(np.arange(NE, dtype=np.float32), (P, NE))
    small = np.concatenate([eye8, eye8 * REG, kscale, p.astype(np.float32)[:, None],
                            np.repeat(p[:, None], NE, axis=1), np.repeat(p[:, None] + P, NE, axis=1)], axis=1)
    square = np.concatenate([ident, mask, tri, np.ones((P, P), np.float32)], axis=1)
    chunk = np.arange(NCH)
    dest = (np.arange(2)[None, :, None] * NTOK + chunk[None, None, :] * P + p[:, None, None]).astype(np.int32)
    return {
        "c_square": np.ascontiguousarray(square),
        "c_qdecay": np.ascontiguousarray(qdecay),
        "c_small": np.ascontiguousarray(small.astype(np.float32)),
        "c_dest": np.ascontiguousarray(dest.reshape(P, 2 * NCH)),
    }


class Step:

    def __init__(self, turn, place, unroll):
        self.turn, self.place, self.unroll = turn + place // unroll, place % unroll, unroll

    def back(self, k):
        return Step(self.turn, self.place - k, self.unroll)

    @property
    def n(self):
        return self.turn * self.unroll + self.place

    def exists(self, count):
        return not isinstance(self.turn, int) or 0 <= self.n < count


def at_least(engine, sem, value):
    if not isinstance(value, int) or value > 0:
        engine.wait_ge(sem, value)


def settle(engine):
    engine.nop(nofuse=True)


def run_steps(engine, count, extra, unroll, body, behind={}):
    for place in range(unroll):
        body(Step(0, place, unroll))
        if place in behind:
            behind[place]()
    with engine.Fori(1, count // unroll) as turn:
        for place in range(unroll):
            body(Step(turn, place, unroll))
    for n in range(count, count + extra):
        body(Step(n // unroll, n % unroll, unroll))



def build(nc, x, Wq, Wk, Wv, Wo, gate, M0, Wg, bg, W1, b1, W2, b2, c, wmod,
          c_square, c_qdecay, c_small, c_dest, out, routed, y_rows, bias_rows):
    with ExitStack() as ctx:
        def sb(name, shape, dt=F32):
            return ctx.enter_context(nc.sbuf_tensor(name, shape, dt))

        def sem(name):
            return ctx.enter_context(nc.semaphore(name))

        bank = [ctx.enter_context(nc.psum_tensor(f"bank{i}", [P, 512], F32)) for i in range(8)]

        X = sb("X", [P, NCH, D])
        W1h = sb("W1h", [P, NE * DFF], F32R)
        W1l = sb("W1l", [P, NE * DFF], F32R)
        W2hl = sb("W2hl", [P, NE * FB, 2 * D], F32R)
        B1 = sb("B1", [P, NE * DFF], F32R)
        B2 = sb("B2", [P, NE * D], F32R)
        onesR = sb("onesR", [P, P], F32R)
        square = sb("square", [P, 4 * P])
        ident = square[:, 0:P]
        small = sb("small", [P, 4 * NE + 2])
        expert_id, expert_base = small[:, 0:NE], small[:, NE:2 * NE]
        kscale, pid = small[:, 2 * NE:2 * NE + 1], small[:, 2 * NE + 1:2 * NE + 2]
        tile_id = small[:, 2 * NE + 2:].rearrange("p (h e) -> p h e", h=2)
        qdecay = sb("qdecay", [MEM, BC * P])
        dest = sb("dest", [P, 2, NCH], I32)
        tri = sb("tri", [P, P], BF16)
        ones = sb("ones", [P, P], BF16)
        mod = sb("mod", [P, 6, D])
        wqk = sb("wqk", [P, 2 * MEM])
        wvo = sb("wvo", [P, D])
        WgS = sb("WgS", [P, NE])
        bgS = sb("bgS", [P, NE])
        top = sb("top", [P, NCH, 8])
        pairw = sb("pairw", [P, 2, NCH])
        stage = sb("stage", [P, 2, HALF])
        cS = sb("cS", [NB, 3, D])
        scT = sb("scT", [P, P])
        wsm = sb("wsm", [P, 3 * D + MEM + 1])
        woT = sb("woT", [MEM, D])
        M0S = sb("M0S", [MEM, MEM])
        bS = sb("bS", [P, MEM + NE])
        bH = sb("bH", [P, MEM + NE], F32R)
        bL = sb("bL", [P, MEM + NE], F32R)
        hn = sb("hn", [P, 2, BC, D])
        wmS = hn[:].rearrange("p a c d -> p (a c d)")[:, 0:6 * D]
        hT = sb("hT", [P, BC * P])
        qT = sb("qT", [MEM, 2, BC * P])
        kT = sb("kT", [MEM, 2, BC * P])
        vS = sb("vS", [P, 2, BC, D])
        kS = sb("kS", [P, 2, BC, MEM])
        aS = sb("aS", [P, BC, P])
        att = sb("att", [P, BC, D])
        Mst = sb("Mst", [MEM, 2, BC, D])
        st6 = sb("st6", [P, BC, 6])
        mv = sb("mv", [P, BC, 2])
        rs = sb("rs", [P, 8, BC])
        rows = sb("rows", [P, 2, 2, BC, ROWW])
        h2T = sb("h2T", [P, BC * P])
        lg = sb("lg", [P, BC, NE])
        rs8 = sb("sorted8", [P, BC, 8])
        chosen = sb("chosen", [P, BC, 8], U32)
        chosen_f = sb("chosen_f", [P, BC, 8])
        oh = sb("oh", [P, 2, BC, NE])
        T = sb("T", [P, BC, NE], BF16)
        cum = sb("cum", [P, 2, NE])
        cumb = sb("cumb", [P, NE], BF16)
        rk = sb("rk", [P, BC, NE])
        rk2 = sb("rk2", [P, 2, BC, NE])
        posf = sb("posf", [P, 2 * BC])
        pos = sb("pos", [P, 2, 2 * BC], I32)
        padrow = sb("padrow", [P, ROWW])
        padpos = sb("padpos", [P, NE + 1], I32)
        padf = sb("padf", [P, NE + 1])
        cnt_i = sb("cnt_i", [P, NE], I32)
        tiles_f = sb("tiles_f", [P, 3, NE])
        beyond = sb("beyond", [P, 2, 2, NE])
        tab = sb("tab", [P, 3, 2])
        tile_row = sb("tile_row", [1, NTILE], I32)
        tile_exp = sb("tile_exp", [1, NTILE], I32)
        tin = rows[:, 0, 0]
        th = sb("th", [P, 2, P], F32R)
        tl = sb("tl", [P, 2, P], F32R)
        g = stage[:, 0, 0:2 * DFF].rearrange("p (b f) -> p b f", b=2)
        gh = sb("gh", [P, 2, DFF], F32R)
        gl = sb("gl", [P, 2, DFF], F32R)
        ysb = att
        yb = stage[:, 1, :].rearrange("p (b k c d) -> p b k c d", b=2, k=2, c=BC)[:, :, :, :, :]

        S = {n: sem(n) for n in (
            "consts_in", "wmod_in", "w1_in0", "w1_in1", "w2_in0", "w2_in1", "biases_split", "biases_out", "biases_in", "act_setup",
            "silu_ready", "transposed", "copied", "products", "setup_done", "split_hi", "split_lo", "zeroed",
            "ln1_var", "ln1_sd", "ln2_var", "ln2_sd", "h_ready", "hT_ps", "hT_ready", "qk_ps", "v_ps",
            "q_ready", "k_ready", "v_ready", "s_ps", "a_ready", "u_ps", "m_ready", "o_ps", "o_read",
            "h2_ready", "h2_copied", "dest_set", "h2T_ps", "h2T_ready", "lg_ps", "t_ready", "rk_ps", "pos_ready",
            "dve", "cum_ready", "cnt_ps", "tab_cols", "tab_ps", "pads_ready", "pads_in", "table_ready",
            "exp_in", "exp_ready", "w_ready",
            "th_ps", "th_ready", "mm1", "gelu", "gt_ps", "gh_ready", "gl_ready", "y_ps", "y_ready",
            "y0_scaled", "y_weighted", "y_summed", "sum_ready", "out_done",
        )}
        x_in = [sem(f"x_in{i}") for i in range(2)]
        rows_out = [sem(f"rows_out{i}") for i in range(2)]
        tile_in = [sem(f"tile_in{i}") for i in range(SLOTS)]
        tile_out = [sem(f"tile_out{i}") for i in range(SLOTS)]
        y_in = [sem(f"y_in{i}") for i in range(2)]

        x_v = x.rearrange("b (n c t) d -> n t b c d", c=BC, t=TI)
        out_v = out.rearrange("b (n c t) d -> n t b c d", c=BC, t=TI)
        y_v = y_rows.rearrange("(k n c p) d -> k n p c d", k=2, p=P, c=BC)

        def chunk(n, j):
            return X[:, bass.ds(n.n * BC + j, 1), :].rearrange("p a d -> p (a d)")

        def group(n):
            return X[:, bass.ds(n.n * BC, BC), :]

        loads = ((square[:], c_square), (small[:], c_small), (cS[:, 0, :], c), (WgS[:], Wg), (M0S[:], M0),
                 (bgS[:], bg.rearrange("(a e) -> a e", a=1).broadcast_to((P, NE))),
                 (wsm[0:MEM, 0:D], Wq), (wsm[0:MEM, D:2 * D], Wk), (wsm[0:MEM, 2 * D:3 * D], Wv),
                 (wsm[:, 3 * D:3 * D + MEM], Wo),
                 (wsm[:, 3 * D + MEM:], gate.rearrange("(a e) -> a e", a=1).broadcast_to((P, 1))),
                 (bS[:, 0:MEM], b1.rearrange("e (q f) -> (e q) f", f=MEM)),
                 (bS[:, MEM:], b2.rearrange("e (q f) -> (e q) f", f=NE)),
                 (qdecay[:], c_qdecay), (dest[:].rearrange("p k c -> p (k c)"), c_dest))
        CONSTS = 16 * len(loads)

        block = ctx.enter_context(nc.Block())

        @block.sync
        def _(sp):
            for dst, src in loads:
                sp.dma_start(dst, src).then_inc(S["consts_in"], 16)
            sp.dma_start(wmS, wmod).then_inc(S["wmod_in"], 16)

            def load_x(n):
                at_least(sp, S["hT_ps"], n.n - 1)
                settle(sp)
                for t in range(TI):
                    sp.dma_start(X[t * NB:(t + 1) * NB, bass.ds(n.n * BC, BC), :], x_v[n.n, t]).then_inc(
                        x_in[n.place], 16)

            load_x(Step(0, 0, 2))
            load_x(Step(0, 1, 2))
            HE = NE // 2
            w1_v, w2_v = W1.rearrange("e d f -> d e f"), W2.rearrange("e (f p) d -> p e f d", p=P)
            for i in range(2):
                sp.dma_start(stage[:, i, :].rearrange("p (e f) -> p e f", e=HE),
                             w1_v[:, i * HE:(i + 1) * HE]).then_inc(S[f"w1_in{i}"], 16)
            sp.wait_ge(S["biases_split"], 2)
            for i, part in enumerate((bH, bL)):
                sp.dma_start(bias_rows[i, 0:NE * DFF].rearrange("(p f) -> p f", p=P),
                             part[:, 0:MEM].bitcast(F32)).then_inc(S["biases_out"], 16)
                sp.dma_start(bias_rows[i, NE * DFF:].rearrange("(p f) -> p f", p=P),
                             part[:, MEM:].bitcast(F32)).then_inc(S["biases_out"], 16)
            for i in range(2):
                sp.wait_ge(S["split_lo"], i + 1)
                sp.dma_start(stage[:, i, :].rearrange("p (e f d) -> p e f d", e=HE, f=FB),
                             w2_v[:, i * HE:(i + 1) * HE]).then_inc(S[f"w2_in{i}"], 16)
            with sp.Fori(1, NG // 2) as turn:
                load_x(Step(turn, 0, 2))
                load_x(Step(turn, 1, 2))
            sp.wait_ge(S["biases_out"], 64)
            sp.wait_ge(S["zeroed"], 3)
            for i in range(2):
                sp.dma_start(B1[32 * i:32 * i + 1, :].bitcast(F32),
                             bias_rows[i:i + 1, 0:NE * DFF]).then_inc(S["biases_in"], 16)
                sp.dma_start(B2[32 * i:32 * i + 1, :].bitcast(F32),
                             bias_rows[i:i + 1, NE * DFF:]).then_inc(S["biases_in"], 16)

            sp.wait_ge(S["table_ready"], 2)
            sp.wait_ge(S["pads_in"], 16 * (NE + 1))
            for s in range(2):
                sp.wait_ge(rows_out[s], 16 * 2 * BC * NG // 2)

            def load_tile(j):
                at_least(sp, S["th_ps"], j.n - SLOTS + 1)
                settle(sp)
                at_least(sp, tile_out[j.place], j.turn * 16)
                settle(sp)
                row = sp.value_load(tile_row[0:1, bass.ds(j.n, 1)], min_val=0, max_val=PAD_ROW)
                sp.dma_start(tin[:, j.place, :], routed[bass.ds(row, P), :]).then_inc(tile_in[j.place], 16)
            run_steps(sp, NTILE, 0, SLOTS, load_tile)

            for s in range(SLOTS):
                sp.wait_ge(tile_out[s], 16 * NTILE // SLOTS)

            def load_y(n):
                at_least(sp, S["sum_ready"], n.n - 1)
                settle(sp)
                for k in range(2):
                    sp.dma_start(yb[:, n.place, k], y_v[k, n.n]).then_inc(y_in[n.place], 16)
            run_steps(sp, NG, 0, 2, load_y)

        @block.gpsimd
        def _(pool):
            pool.memset(B1[:].bitcast(F32), 0.0).then_inc(S["zeroed"], 1)
            pool.memset(B2[:].bitcast(F32), 0.0).then_inc(S["zeroed"], 1)
            pool.memset(padrow[:, 0:D], 0.0).then_inc(S["zeroed"], 1)
            pool.memset(padrow[:, D:].bitcast(I32), SKIP).then_inc(S["zeroed"], 1)
            pool.memset(rows[:, :, :, :, D + 1:], 0.0).then_inc(S["zeroed"], 1)
            for i in range(2):
                pool.wait_ge(S["split_hi"], i + 1)
                cols = slice(i * HALF, (i + 1) * HALF)
                pool.tensor_tensor(W1l[:, cols], stage[:, i, :], W1h[:, cols].bitcast(F32), ALU.subtract).then_inc(
                    S["split_lo"], 1)
            for i in range(2):
                pool.wait_ge(S["split_hi"], i + 3)
                part = W2hl[:, i * NE * FB // 2:(i + 1) * NE * FB // 2, :]
                pool.tensor_tensor(part[:, :, D:2 * D], stage[:, i, :].rearrange("p (e d) -> p e d", d=D),
                                   part[:, :, 0:D].bitcast(F32), ALU.subtract).then_inc(S["split_lo"], 1)

            def scatter(n):
                pool.wait_ge(S["pos_ready"], n.n + 1)
                pool.wait_ge(S["dest_set"], n.n + 1)
                pool.wait_ge(S["h2_ready"], n.n + 1)
                pool.wait_ge(S["h2_copied"], n.n + 1)
                settle(pool)
                for k in range(2):
                    for j in range(BC):
                        pool.indirect_dma_start(
                            routed, bass.IndirectOffsetOnAxis(pos[:, n.place, k * BC + j:k * BC + j + 1], 0),
                            rows[:, n.place, k, j, :], None).then_inc(rows_out[n.place], 16)
            run_steps(pool, NG, 0, 2, scatter)

            pool.wait_ge(S["pads_ready"], 1)
            for e in range(NE + 1):
                pool.indirect_dma_start(
                    routed, bass.IndirectOffsetOnAxis(padpos[:, e:e + 1], 0), padrow[:], None).then_inc(
                        S["pads_in"], 16)

            def put_y(j):
                pool.wait_ge(S["y_ready"], j.n + 1)
                settle(pool)
                pool.indirect_dma_start(
                    y_rows, bass.IndirectOffsetOnAxis(tin[:, j.place, D:D + 1].bitcast(I32), 0),
                    ysb[:, j.place, :], None, bounds_check=2 * NTOK - 1, oob_is_err=False).then_inc(
                        tile_out[j.place], 16)
            run_steps(pool, NTILE, 0, SLOTS, put_y)

            def add_x(n):
                pool.wait_ge(S["y_summed"], n.n + 1)
                settle(pool)
                pool.tensor_tensor(group(n), group(n), yb[:, n.place, 0], ALU.add).then_inc(S["sum_ready"], 1)
            run_steps(pool, NG, 0, 2, add_x)

        @block.scalar
        def _(act):
            act.wait_ge(S["consts_in"], CONSTS)
            act.activation(cS[:, 1, :], cS[:, 0, :], ACT.Exp, scale=-1.0).then_inc(S["act_setup"], 1)
            act.activation(wsm[:, 3 * D + MEM:], wsm[:, 3 * D + MEM:], ACT.Exp, scale=-1.0).then_inc(
                S["act_setup"], 1)

            def front(n):
                act.wait_ge(S["ln1_var"], n.n + 1)
                act.activation(rs[:, 1, :], rs[:, 0, :], ACT.Sqrt).then_inc(S["ln1_sd"], 1)
                act.wait_ge(S["hT_ps"], n.n + 1)
                at_least(act, S["v_ps"], n.n)
                act.activation(hT[:], bank[0][:], ACT.Copy).then_inc(S["hT_ready"], 1)
                act.wait_ge(S["qk_ps"], n.n + 1)
                at_least(act, S["s_ps"], n.n - 1)
                act.activation(kT[:, n.place, :], bank[1][MEM:2 * MEM, :], ACT.Copy).then_inc(S["k_ready"], 1)
                act.wait_ge(S["v_ps"], n.n + 1)
                at_least(act, S["o_ps"], n.n - 1)
                act.activation(vS[:, n.place], bank[3][:].rearrange("p (c d) -> p c d", c=BC), ACT.Copy).then_inc(
                    S["v_ready"], 1)
                act.activation(kS[:, n.place], bank[2][:, 0:BC * MEM].rearrange("p (c d) -> p c d", c=BC),
                               ACT.Copy, scale=kscale).then_inc(S["v_ready"], 1)

            def middle(n):
                act.wait_ge(S["ln2_var"], n.n + 1)
                act.activation(rs[:, 5, :], rs[:, 4, :], ACT.Sqrt).then_inc(S["ln2_sd"], 1)
                act.wait_ge(S["h2_ready"], n.n + 1)
                at_least(act, rows_out[n.place], n.turn * (2 * BC * 16))
                act.activation(rows[:, n.place, 1, :, 0:D], rows[:, n.place, 0, :, 0:D], ACT.Copy).then_inc(
                    S["h2_copied"], 1)

            def last(n):
                act.wait_ge(S["h2T_ps"], n.n + 1)
                at_least(act, S["lg_ps"], n.n)
                act.activation(h2T[:], bank[7][:], ACT.Copy).then_inc(S["h2T_ready"], 1)

            def steps(n):
                if n.back(2).exists(NG):
                    last(n.back(2))
                if n.exists(NG):
                    front(n)
                if n.back(1).exists(NG):
                    middle(n.back(1))

            def split_w1():
                for i in range(2):
                    act.wait_ge(S[f"w1_in{i}"], 16)
                    act.activation(W1h[:, i * HALF:(i + 1) * HALF], stage[:, i, :], ACT.Copy).then_inc(
                        S["split_hi"], 1)

            def split_w2():
                for i in range(2):
                    act.wait_ge(S[f"w2_in{i}"], 16)
                    act.activation(W2hl[:, i * NE * FB // 2:(i + 1) * NE * FB // 2, 0:D],
                                   stage[:, i, :].rearrange("p (e d) -> p e d", d=D), ACT.Copy).then_inc(
                                       S["split_hi"], 1)

            run_steps(act, NG, 2, 2, steps, {0: split_w1, 1: split_w2})
            act.wait_ge(S["exp_in"], 1)
            act.activation(pairw[:, 1, :], pairw[:, 0, :], ACT.Exp).then_inc(S["exp_ready"], 1)

            def tile(n):
                j = n.back(1)
                if j.exists(NTILE):
                    act.wait_ge(S["mm1"], j.n + 1)
                    at_least(act, S["gt_ps"], j.n - 1)
                    act.activation(g[:, j.place % 2, :], bank[2 + j.place % 2][:], ACT.Gelu).then_inc(S["gelu"], 1)
                j = n.back(2)
                if j.exists(NTILE):
                    act.wait_ge(S["gt_ps"], j.n + 1)
                    at_least(act, S["y_ps"], j.n - 1)
                    act.activation(gh[:, j.place % 2, :], bank[4 + j.place % 2][:], ACT.Copy).then_inc(
                        S["gh_ready"], 1)
            act.wait_ge(S["split_lo"], 4)
            run_steps(act, NTILE, 2, SLOTS, tile)

            def end(n):
                if n.exists(NG):
                    act.wait_ge(y_in[n.place], (n.turn + 1) * 32)
                    settle(act)
                    for j in range(BC):
                        ins = act.activation(yb[:, n.place, 0, j, :], yb[:, n.place, 0, j, :], ACT.Copy,
                                             scale=pairw[:, 0, bass.ds(n.n * BC + j, 1)])
                    ins.then_inc(S["y0_scaled"], 1)
                m = n.back(1)
                if m.exists(NG):
                    act.wait_ge(S["sum_ready"], m.n + 1)
                    settle(act)
                    for t in range(TI):
                        act.dma_start(out_v[m.n, t], X[t * NB:(t + 1) * NB, bass.ds(m.n * BC, BC), :]).then_inc(
                            S["out_done"], 16)
            act.wait_ge(S["w_ready"], 1)
            run_steps(act, NG, 1, 2, end)
            act.wait_ge(S["out_done"], 16 * TI * NG)

        @block.vector
        def _(dve):
            chain = [0, 0]

            def mark(ins):
                chain[0] += 1
                ins.then_inc(S["dve"], 1)

            def then(ins):
                mark(ins)
                dve.wait_ge(S["dve"], chain[1] + chain[0])

            dve.wait_ge(S["consts_in"], CONSTS)
            mark(dve.tensor_copy(tri[:], square[:, 2 * P:3 * P]))
            mark(dve.tensor_copy(ones[:], square[:, 3 * P:4 * P]))
            mark(dve.tensor_copy(onesR[:], square[:, 3 * P:4 * P]))
            dve.tensor_copy(bH[:], bS[:]).then_inc(S["biases_split"], 1)
            dve.wait_ge(S["biases_split"], 1)
            dve.tensor_tensor(bL[:], bS[:], bH[:].bitcast(F32), ALU.subtract).then_inc(S["biases_split"], 1)
            dve.wait_ge(S["act_setup"], 2)
            gt = wsm[:, 3 * D + MEM:]
            then(dve.tensor_scalar(cS[:, 2, :], cS[:, 1, :], 1.0, None, ALU.add))
            then(dve.reciprocal(cS[:, 1, :], cS[:, 2, :]))
            dve.tensor_tensor(cS[:, 2, :], cS[:, 1, :], cS[:, 0, :], ALU.mult).then_inc(S["silu_ready"], 1)
            then(dve.tensor_scalar(gt, gt, 1.0, None, ALU.add))
            then(dve.reciprocal(gt, gt))
            dve.wait_ge(S["transposed"], 1)
            dve.tensor_copy(scT[:].rearrange("p (t b) -> p t b", t=TI),
                            bank[0][:, 0:NB].rearrange("p (t b) -> p t b", t=1).broadcast_to(
                                (P, TI, NB))).then_inc(S["copied"], 1)
            dve.tensor_copy(wqk[:], bank[0][:, NB:NB + 2 * MEM]).then_inc(S["copied"], 1)
            dve.tensor_copy(woT[:], bank[0][0:MEM, P:P + D]).then_inc(S["copied"], 1)
            dve.wait_ge(S["products"], 1)
            then(dve.memset(cum[:], 0.0))
            mark(dve.memset(cumb[:], 0.0))
            mark(dve.tensor_copy(wvo[:], bank[2][:, 0:D]))
            mark(dve.tensor_copy(Mst[:, 0, 0, :], bank[3][0:MEM, 0:D]))
            mark(dve.tensor_copy(mod[:, 0:3, :], bank[4][:, 0:3 * D].rearrange("p (s d) -> p s d", s=3)))
            then(dve.tensor_copy(mod[:, 3:6, :], bank[5][:, 0:3 * D].rearrange("p (s d) -> p s d", s=3)))
            for i in (1, 4):
                then(dve.tensor_scalar(mod[:, i, :], mod[:, i, :], 1.0, None, ALU.add))
            for i in (2, 5):
                mark(dve.tensor_scalar(att[:, 0, :], mod[:, i, :], 0.0, 2.0, ALU.is_ge, ALU.mult))
                then(dve.tensor_scalar(att[:, 2, :], mod[:, i, :], -1.0, 0.25, ALU.mult, ALU.max))
                then(dve.tensor_tensor(att[:, 1, :], mod[:, i, :], att[:, 2, :], ALU.max))
                then(dve.scalar_tensor_tensor(out=mod[:, i, :], in0=att[:, 0, :], scalar=-1.0, in1=att[:, 1, :],
                                              op0=ALU.add, op1=ALU.mult))
            dve.tensor_scalar(mod[:, 2, :], mod[:, 2, :], gt, None, ALU.mult).then_inc(S["setup_done"], 1)
            dve.wait_ge(S["setup_done"], 1)

            def per_token(i):
                return mod[:, i:i + 1, :].broadcast_to((P, BC, D))

            def norm(n, var_sem, sd_sem, base, scale, shift, last_sem, dst):
                for j in range(BC):
                    mark(dve.bn_stats(st6[:, j, :], chunk(n, j)))
                dve.wait_ge(S["dve"], chain[1] + chain[0])
                settle(dve)
                for j in range(BC):
                    mark(dve.bn_aggr(mv[:, j, :], st6[:, j, :]))
                dve.wait_ge(S["dve"], chain[1] + chain[0])
                v, sd, r, t = (rs[:, base + i, :] for i in range(4))
                dve.tensor_scalar(v, mv[:, :, 1], EPS, None, ALU.add).then_inc(S[var_sem], 1)
                dve.wait_ge(S[sd_sem], n.n + 1)
                then(dve.reciprocal(r, sd))
                then(dve.tensor_tensor(t, r, r, ALU.mult))
                then(dve.tensor_tensor(t, t, v, ALU.mult))
                then(dve.tensor_scalar(t, t, -0.5, 1.5, ALU.mult, ALU.add))
                then(dve.tensor_tensor(r, r, t, ALU.mult))
                for j in range(BC):
                    mark(dve.tensor_scalar(dst[:, j, :], chunk(n, j), mv[:, j, 0:1], r[:, j:j + 1],
                                           ALU.subtract, ALU.mult))
                dve.wait_ge(S["dve"], chain[1] + chain[0])
                then(dve.tensor_tensor(dst, dst, per_token(scale), ALU.mult))
                dve.tensor_tensor(dst, dst, per_token(shift), ALU.add).then_inc(S[last_sem], 1)

            def norm1(n):
                dve.wait_ge(x_in[n.place], (n.turn + 1) * (TI * 16))
                at_least(dve, S["hT_ps"], n.n - 1)
                settle(dve)
                norm(n, "ln1_var", "ln1_sd", 0, 1, 0, "h_ready", hn[:, n.place])

            def scores(n):
                dve.wait_ge(S["s_ps"], n.n + 1)
                at_least(dve, S["o_ps"], n.n)
                dve.tensor_tensor(aS[:], bank[4][:].rearrange("p (c t) -> p c t", c=BC),
                                  square[:, P:2 * P].rearrange("p (a t) -> p a t", a=1).broadcast_to((P, BC, P)),
                                  ALU.mult).then_inc(S["a_ready"], 1)

            def states(n):
                dve.wait_ge(S["u_ps"], n.n + 1)
                for j in range(BC):
                    to = Mst[:, n.place, j + 1, :] if j < BC - 1 else Mst[:, 1 - n.place, 0, :]
                    dve.scalar_tensor_tensor(out=to, in0=Mst[:, n.place, j, :], scalar=DECAY ** TI,
                                             in1=bank[5][0:MEM, j * D:(j + 1) * D], op0=ALU.mult,
                                             op1=ALU.add).then_inc(S["m_ready"], 1)
                    dve.wait_ge(S["m_ready"], n.n * BC + j + 1)

            def queries(n):
                dve.wait_ge(S["qk_ps"], n.n + 1)
                at_least(dve, S["o_ps"], n.n - 1)
                dve.tensor_tensor(qT[:, n.place, :], bank[1][0:MEM, :], qdecay[:], ALU.mult).then_inc(
                    S["q_ready"], 1)

            def residual(n):
                dve.wait_ge(S["o_ps"], n.n + 1)
                dve.tensor_tensor(att[:], bank[4][:].rearrange("p (c d) -> p c d", c=BC), per_token(2),
                                  ALU.mult).then_inc(S["o_read"], 1)
                dve.wait_ge(S["o_read"], n.n + 1)
                then(dve.tensor_tensor(group(n), group(n), att[:], ALU.add))

            def norm2(n):
                at_least(dve, rows_out[n.place], n.turn * (2 * BC * 16))
                at_least(dve, S["h2T_ps"], n.n - 1)
                settle(dve)
                norm(n, "ln2_var", "ln2_sd", 4, 4, 3, "h2_ready", rows[:, n.place, 0, :, 0:D])
                for k in range(2):
                    ins = dve.tensor_copy(rows[:, n.place, k, :, D:D + 1].bitcast(I32).rearrange("p c a -> p (c a)"),
                                          dest[:, k, bass.ds(n.n * BC, BC)])
                ins.then_inc(S["dest_set"], 1)

            def choose(n):
                dve.wait_ge(S["lg_ps"], n.n + 1)
                then(dve.tensor_tensor(lg[:], bank[6][:, 0:BC * NE].rearrange("p (c e) -> p c e", c=BC),
                                       bgS[:].rearrange("p (a e) -> p a e", a=1).broadcast_to((P, BC, NE)), ALU.add))
                settle(dve)
                tops = [rs8[:, j, :] for j in range(BC)]
                for j in range(BC):
                    mark(dve.max(tops[j], lg[:, j, :]))
                dve.wait_ge(S["dve"], chain[1] + chain[0])
                settle(dve)
                for j in range(BC):
                    mark(dve.max_index(chosen[:, j, :], tops[j], lg[:, j, :]))
                mark(dve.tensor_copy(top[:, bass.ds(n.n * BC, BC), :], rs8[:]))
                dve.wait_ge(S["dve"], chain[1] + chain[0])
                then(dve.tensor_copy(chosen_f[:], chosen[:]))
                for k in range(2):
                    mark(dve.tensor_tensor(oh[:, k], chosen_f[:, :, k:k + 1].broadcast_to((P, BC, NE)),
                                           expert_id.rearrange("p (a e) -> p a e", a=1).broadcast_to((P, BC, NE)),
                                           ALU.is_equal))
                dve.wait_ge(S["dve"], chain[1] + chain[0])
                dve.tensor_tensor(T[:], oh[:, 0], oh[:, 1], ALU.add).then_inc(S["t_ready"], 1)

            def place(n):
                dve.wait_ge(S["rk_ps"], n.n + 1)
                mark(dve.tensor_reduce(cum[:, 1, :], T[:].rearrange("p c e -> p e c"), AX_X, ALU.add))
                then(dve.tensor_tensor(rk[:], bank[6][:, P:P + BC * NE].rearrange("p (c e) -> p c e", c=BC),
                                       expert_base.rearrange("p (a e) -> p a e", a=1).broadcast_to((P, BC, NE)),
                                       ALU.add))
                mark(dve.tensor_tensor(cum[:, 0, :], cum[:, 0, :], cum[:, 1, :], ALU.add))
                for k in range(2):
                    mark(dve.tensor_tensor(rk2[:, k], rk[:], oh[:, k], ALU.mult))
                dve.wait_ge(S["dve"], chain[1] + chain[0])
                dve.tensor_copy(cumb[:], cum[:, 0, :]).then_inc(S["cum_ready"], 1)
                then(dve.tensor_reduce(posf[:], rk2[:].rearrange("p k c e -> p (k c) e"), AX_X, ALU.add))
                at_least(dve, rows_out[n.place], n.turn * (2 * BC * 16))
                dve.tensor_copy(pos[:, n.place, :], posf[:]).then_inc(S["pos_ready"], 1)

            def steps(n):
                if n.exists(NG):
                    norm1(n)
                m = n.back(1)
                if m.exists(NG):
                    scores(m)
                    states(m)
                if n.exists(NG):
                    queries(n)
                if m.exists(NG):
                    residual(m)
                    norm2(m)
                if n.back(2).exists(NG):
                    choose(n.back(2))
                    place(n.back(2))

            steps(Step(0, 0, 2))
            steps(Step(0, 1, 2))
            before = chain[0]
            NORM = 2 * BC + 5 + BC + 1
            CHOOSE = 1 + 2 * BC + 1 + 1 + 2
            PLACE = 1 + 1 + 1 + 2 + 1
            per_turn = 2 * (2 * NORM + 1 + CHOOSE + PLACE)
            with dve.Fori(1, NG // 2) as turn:
                chain[:] = [0, turn * per_turn + (before - per_turn)]
                steps(Step(turn, 0, 2))
                steps(Step(turn, 1, 2))
                assert chain[0] == per_turn, (chain[0], per_turn)
            chain[:] = [before + (NG // 2 - 1) * per_turn, 0]
            steps(Step(NG // 2, 0, 2))
            steps(Step(NG // 2, 1, 2))

            dve.wait_ge(S["cnt_ps"], 1)
            cnt = bank[6][:, 2 * P:2 * P + NE]
            mark(dve.memset(padf[:, NE:NE + 1], float(PAD_ROW)))
            then(dve.tensor_tensor(padf[:, 0:NE], cnt, expert_base, ALU.add))
            mark(dve.tensor_scalar(cnt_i[:], cnt, float(P - 1), None, ALU.add))
            then(dve.tensor_scalar(padf[:], padf[:], pid, None, ALU.add))
            dve.wait_ge(S["zeroed"], 5)
            dve.tensor_copy(padpos[:], padf[:]).then_inc(S["pads_ready"], 1)
            tiles, upto, jump = tiles_f[:, 0, :], tiles_f[:, 1, :], tiles_f[:, 2, :]
            then(dve.tensor_scalar(cnt_i[:], cnt_i[:], 7, None, ALU.logical_shift_right))
            then(dve.tensor_copy(tiles, cnt_i[:]))
            mark(dve.tensor_scalar(jump, tiles, float(-P), float(REG), ALU.mult, ALU.add))
            then(dve.tensor_tensor_scan(upto, square[:, 3 * P:3 * P + NE], tiles, 0.0, ALU.mult, ALU.add))
            then(dve.tensor_tensor(beyond[:, 0], tile_id, upto.rearrange("p (a e) -> p a e", a=1).broadcast_to(
                (P, 2, NE)), ALU.is_ge))
            then(dve.tensor_tensor(beyond[:, 1], beyond[:, 0], jump.rearrange("p (a e) -> p a e", a=1).broadcast_to(
                (P, 2, NE)), ALU.mult))
            mark(dve.tensor_reduce(tab[:, 0, :], beyond[:, 0], AX_X, ALU.add))
            then(dve.tensor_reduce(tab[:, 1, :], beyond[:, 1], AX_X, ALU.add))
            mark(dve.tensor_scalar(tab[:, 0, :], tab[:, 0, :], float(NE - 1), None, ALU.min))
            then(dve.scalar_tensor_tensor(out=tab[:, 1, :], in0=tile_id[:, :, 0], scalar=float(P), in1=tab[:, 1, :],
                                          op0=ALU.mult, op1=ALU.add))
            dve.tensor_scalar(tab[:, 1, :], tab[:, 1, :], float(PAD_ROW), None, ALU.min).then_inc(S["tab_cols"], 1)
            dve.tensor_tensor(pairw[:, 0, :], top[:, :, 1], top[:, :, 0], ALU.subtract).then_inc(S["exp_in"], 1)
            dve.wait_ge(S["tab_ps"], 1)
            dve.tensor_copy(tile_exp[:], bank[0][0:1, 0:NTILE]).then_inc(S["table_ready"], 1)
            dve.tensor_copy(tile_row[:], bank[0][0:1, 2 * P:2 * P + NTILE]).then_inc(S["table_ready"], 1)
            dve.wait_ge(S["exp_ready"], 1)
            then(dve.tensor_scalar(pairw[:, 0, :], pairw[:, 1, :], 1.0, None, ALU.add))
            then(dve.reciprocal(pairw[:, 0, :], pairw[:, 0, :]))
            dve.tensor_tensor(pairw[:, 1, :], pairw[:, 1, :], pairw[:, 0, :], ALU.mult).then_inc(S["w_ready"], 1)

            def tile(n):
                j, b = n, n.place % 2
                if j.exists(NTILE):
                    dve.wait_ge(S["th_ps"], j.n + 1)
                    at_least(dve, S["mm1"], j.n - 1)
                    dve.tensor_copy(th[:, b, :], bank[b][:, 0:P]).then_inc(S["th_ready"], 1)
                    dve.wait_ge(S["th_ready"], j.n * 2 + 1)
                    dve.tensor_tensor(tl[:, b, :], bank[b][:, 0:P], th[:, b, :].bitcast(F32),
                                      ALU.subtract).then_inc(S["th_ready"], 1)
                j = n.back(3)
                b = j.place % 2
                if j.exists(NTILE):
                    dve.wait_ge(S["y_ps"], j.n + 1)
                    at_least(dve, tile_out[j.place], j.turn * 16)
                    dve.tensor_reduce(ysb[:, j.place, :],
                                      bank[6 + b][:, 0:2 * D].rearrange("p (h d) -> p d h", h=2), AX_X,
                                      ALU.add).then_inc(S["y_ready"], 1)
                j = n.back(2)
                b = j.place % 2
                if j.exists(NTILE):
                    dve.wait_ge(S["gh_ready"], j.n + 1)
                    at_least(dve, S["y_ps"], j.n - 1)
                    dve.tensor_tensor(gl[:, b, :], bank[4 + b][:], gh[:, b, :].bitcast(F32),
                                      ALU.subtract).then_inc(S["gl_ready"], 1)
            run_steps(dve, NTILE, 3, SLOTS, tile)

            def end(n):
                dve.wait_ge(S["y0_scaled"], n.n + 1)
                settle(dve)
                for j in range(BC):
                    ins = dve.scalar_tensor_tensor(
                        out=yb[:, n.place, 0, j, :], in0=yb[:, n.place, 1, j, :],
                        scalar=pairw[:, 1, bass.ds(n.n * BC + j, 1)], in1=yb[:, n.place, 0, j, :],
                        op0=ALU.mult, op1=ALU.add)
                ins.then_inc(S["y_weighted"], 1)
                dve.wait_ge(S["y_weighted"], n.n + 1)
                dve.tensor_tensor(yb[:, n.place, 0], yb[:, n.place, 0], per_token(5), ALU.mult).then_inc(
                    S["y_summed"], 1)
            dve.wait_ge(S["w_ready"], 1)
            run_steps(dve, NG, 0, 2, end)

        @block.tensor
        def _(pe):
            pe.wait_ge(S["consts_in"], CONSTS)
            pe.transpose(bank[0][:, NB:NB + MEM], wsm[0:MEM, 0:D], ident[0:MEM, 0:MEM])
            pe.transpose(bank[0][:, NB + MEM:NB + 2 * MEM], wsm[0:MEM, D:2 * D], ident[0:MEM, 0:MEM])
            pe.transpose(bank[0][0:MEM, P:P + D], wsm[:, 3 * D:3 * D + MEM], ident)
            pe.wait_ge(S["silu_ready"], 1)
            pe.transpose(bank[0][:, 0:NB], cS[:, 2, :], ident[0:NB, 0:NB]).then_inc(S["transposed"], 1)
            pe.wait_ge(S["copied"], 3)
            pe.wait_ge(S["wmod_in"], 16)
            pe.matmul(bank[2][:, 0:D], wsm[0:MEM, 2 * D:3 * D], woT[:], start=True, stop=True)
            pe.matmul(bank[3][0:MEM, 0:D], M0S[:], woT[:], start=True, stop=True)
            pe.matmul(bank[4][:, 0:3 * D], scT[:], wmS[:, 0:3 * D], start=True, stop=True)
            pe.matmul(bank[5][:, 0:3 * D], scT[:], wmS[:, 3 * D:6 * D], start=True, stop=True).then_inc(
                S["products"], 1)
            pe.wait_ge(S["setup_done"], 1)

            def front(n):
                pe.wait_ge(S["h_ready"], n.n + 1)
                at_least(pe, S["hT_ready"], n.n)
                for j in range(BC):
                    ins = pe.transpose(bank[0][:, j * P:(j + 1) * P], hn[:, n.place, j, :], ident)
                ins.then_inc(S["hT_ps"], 1)
                pe.wait_ge(S["hT_ready"], n.n + 1)
                at_least(pe, S["q_ready"], n.n)
                at_least(pe, S["k_ready"], n.n)
                pe.matmul(bank[1][0:2 * MEM, :], wqk[:], hT[:], start=True, stop=True).then_inc(S["qk_ps"], 1)
                at_least(pe, S["v_ready"], n.n * 2)
                for j in range(BC):
                    pe.matmul(bank[2][:, j * MEM:(j + 1) * MEM], hT[:, j * P:(j + 1) * P], wqk[:, MEM:2 * MEM],
                              start=True, stop=True)
                    ins = pe.matmul(bank[3][:, j * D:(j + 1) * D], hT[:, j * P:(j + 1) * P], wvo[:],
                                    start=True, stop=True)
                ins.then_inc(S["v_ps"], 1)

            def middle(n):
                pe.wait_ge(S["q_ready"], n.n + 1)
                pe.wait_ge(S["k_ready"], n.n + 1)
                at_least(pe, S["o_read"], n.n)
                for j in range(BC):
                    cols = slice(j * P, (j + 1) * P)
                    ins = pe.matmul(bank[4][:, cols], kT[:, n.place, cols], qT[:, n.place, cols],
                                    start=True, stop=True)
                ins.then_inc(S["s_ps"], 1)
                pe.wait_ge(S["v_ready"], n.n * 2 + 2)
                at_least(pe, S["m_ready"], n.n * BC)
                for j in range(BC):
                    ins = pe.matmul(bank[5][0:MEM, j * D:(j + 1) * D], kS[:, n.place, j, :], vS[:, n.place, j, :],
                                    start=True, stop=True)
                ins.then_inc(S["u_ps"], 1)

            def outputs(n):
                pe.wait_ge(S["a_ready"], n.n + 1)
                pe.wait_ge(S["m_ready"], n.n * BC + BC - 1)
                for j in range(BC):
                    cols = slice(j * P, (j + 1) * P)
                    pe.matmul(bank[4][:, cols], aS[:, j, :], vS[:, n.place, j, :], start=True, stop=False)
                    ins = pe.matmul(bank[4][:, cols], qT[:, n.place, cols], Mst[:, n.place, j, :],
                                    start=False, stop=True)
                ins.then_inc(S["o_ps"], 1)

            def logits(n):
                pe.wait_ge(S["h2_ready"], n.n + 1)
                at_least(pe, S["h2T_ready"], n.n)
                for j in range(BC):
                    ins = pe.transpose(bank[7][:, j * P:(j + 1) * P], rows[:, n.place, 0, j, 0:D], ident)
                ins.then_inc(S["h2T_ps"], 1)
                pe.wait_ge(S["h2T_ready"], n.n + 1)
                at_least(pe, S["pos_ready"], n.n)
                for j in range(BC):
                    ins = pe.matmul(bank[6][:, j * NE:(j + 1) * NE], h2T[:, j * P:(j + 1) * P], WgS[:],
                                    start=True, stop=True)
                ins.then_inc(S["lg_ps"], 1)

            def ranks(n):
                pe.wait_ge(S["t_ready"], n.n + 1)
                at_least(pe, S["cum_ready"], n.n)
                r = bank[6][:, P:P + BC * NE].rearrange("p (c e) -> p c e", c=BC)
                pe.matmul(r, ones[:], cumb[:].rearrange("p (a e) -> p a e", a=1).broadcast_to((P, BC, NE)),
                          start=True, stop=False)
                for j in range(BC - 1):
                    pe.matmul(r[:, j + 1:, :], ones[:], T[:, j:j + 1, :].broadcast_to((P, BC - 1 - j, NE)),
                              start=False, stop=False)
                pe.matmul(r, tri[:], T[:], start=False, stop=True).then_inc(S["rk_ps"], 1)

            def steps(n):
                if n.back(1).exists(NG):
                    middle(n.back(1))
                if n.back(2).exists(NG):
                    logits(n.back(2))
                if n.exists(NG):
                    front(n)
                if n.back(1).exists(NG):
                    outputs(n.back(1))
                if n.back(2).exists(NG):
                    ranks(n.back(2))
            run_steps(pe, NG, 2, 2, steps)

            pe.wait_ge(S["cum_ready"], NG)
            pe.matmul(bank[6][:, 2 * P:2 * P + NE], ones[:], cumb[:], start=True, stop=True).then_inc(S["cnt_ps"], 1)
            pe.wait_ge(S["tab_cols"], 1)
            for i in range(2):
                pe.matmul(bank[0][0:1, 2 * P * i:2 * P * i + P], tab[:, i, 0:1], ident, start=True, stop=True)
                ins = pe.matmul(bank[0][0:1, 2 * P * i + P:2 * P * i + NTILE], tab[:, i, 1:2],
                                ident[:, 0:NTILE - P], start=True, stop=True)
            ins.then_inc(S["tab_ps"], 1)
            pe.wait_ge(S["table_ready"], 2)
            pe.wait_ge(S["split_lo"], 4)
            pe.wait_ge(S["biases_in"], 64)

            def expert(j):
                return pe.value_load(tile_exp[0:1, bass.ds(j.n, 1)], min_val=0, max_val=NE - 1)

            def tile(n):
                j, b = n, n.place % 2
                if j.exists(NTILE):
                    pe.wait_ge(tile_in[j.place], (j.turn + 1) * 16)
                    at_least(pe, S["th_ready"], j.n * 2 - 2)
                    pe.transpose(bank[b][:, 0:P], tin[:, j.place, 0:D], ident).then_inc(S["th_ps"], 1)
                j = n.back(1)
                b = j.place % 2
                if j.exists(NTILE):
                    e = expert(j)
                    w = bass.ds(e * DFF, DFF)
                    pe.wait_ge(S["th_ready"], j.n * 2 + 2)
                    at_least(pe, S["gelu"], j.n - 1)
                    pe.matmul(bank[2 + b][:], th[:, b, :], W1h[:, w], start=True, stop=False)
                    pe.matmul(bank[2 + b][:], th[:, b, :], W1l[:, w], start=False, stop=False)
                    pe.matmul(bank[2 + b][:], tl[:, b, :], W1h[:, w], start=False, stop=False)
                    pe.matmul(bank[2 + b][:], onesR[:], B1[:, w], start=False, stop=True).then_inc(S["mm1"], 1)
                j = n.back(2)
                b = j.place % 2
                if j.exists(NTILE):
                    pe.wait_ge(S["gelu"], j.n + 1)
                    at_least(pe, S["gl_ready"], j.n - 1)
                    for f in range(FB):
                        ins = pe.transpose(bank[4 + b][:, f * P:(f + 1) * P], g[:, b, f * P:(f + 1) * P], ident)
                    ins.then_inc(S["gt_ps"], 1)
                j = n.back(3)
                b = j.place % 2
                if j.exists(NTILE):
                    e = expert(j)
                    y = bank[6 + b]
                    pe.wait_ge(S["gl_ready"], j.n + 1)
                    at_least(pe, S["y_ready"], j.n - 1)
                    for f in range(FB):
                        w2 = W2hl[:, bass.ds(e * FB + f, 1), :].rearrange("p a d -> p (a d)")
                        pe.matmul(y[:, 0:2 * D], gh[:, b, f * P:(f + 1) * P], w2, start=(f == 0), stop=False)
                        pe.matmul(y[:, 0:D], gl[:, b, f * P:(f + 1) * P], w2[:, 0:D], start=False, stop=False)
                    pe.matmul(y[:, 0:D], onesR[:], B2[:, bass.ds(e * D, D)], start=False,
                              stop=True).then_inc(S["y_ps"], 1)
            run_steps(pe, NTILE, 3, SLOTS, tile)


_INS = ["L0_attn_x", "L0_attn_Wq", "L0_attn_Wk", "L0_attn_Wv", "L0_attn_Wo", "L0_attn_gate", "L0_attn_M0",
        "L0_ffn_Wg", "L0_ffn_bg", "L0_ffn_W1", "L0_ffn_b1", "L0_ffn_W2", "L0_ffn_b2", "L0_c", "L0_wmod"]


def kernel(**inputs):
    import concourse.bacc as bacc
    from concourse.bass_utils import run_bass_kernel_spmd

    nc = bacc.Bacc("TRN2", target_bir_lowering=False, num_devices=1)
    arrays = {f"in_{name}": np.ascontiguousarray(inputs[name]) for name in _INS}
    arrays.update(shape_constants())
    args = [nc.dram_tensor(name, a.shape, mybir.dt.from_np(a.dtype), kind="ExternalInput").ap()
            for name, a in arrays.items()]
    out = nc.dram_tensor("out_0", (NB, NT, D), F32, kind="ExternalOutput").ap()
    routed = nc.dram_tensor("routed", (NROWS, ROWW), F32, kind="Internal").ap()
    y_rows = nc.dram_tensor("y_rows", (2 * NTOK, D), F32, kind="Internal").ap()
    bias_rows = nc.dram_tensor("bias_rows", (2, NE * (DFF + D)), F32, kind="Internal").ap()
    build(nc, *args, out, routed, y_rows, bias_rows)
    return run_bass_kernel_spmd(nc, [arrays], core_ids=[0]).results[0]["out_0"]
```

```python
from contextlib import ExitStack

import numpy as np
import concourse.bass as bass
from concourse import mybir

F32 = mybir.dt.float32
F32R = mybir.dt.float32r
BF16 = mybir.dt.bfloat16
I32 = mybir.dt.int32
U32 = mybir.dt.uint32
ALU = mybir.AluOpType
ACT = mybir.ActivationFunctionType
AX_X = mybir.AxisListType.X

P = 128
NB = 32
NT = 256
D = 128
MEM = 32
NE = 8
DFF = 512
FB = DFF // P
TI = P // NB
NCH = NT // TI
BC = 4
NG = NCH // BC
NTOK = NB * NT
REG = NTOK + P
ROWW = 132
PAD_ROW = NE * REG
NROWS = PAD_ROW + P
NTILE = 2 * NTOK // P + NE
HALF = NE * DFF // 2
RB = 3
SLOTS = 8
SKIP = 1 << 20
DECAY = 0.99
EPS = 1e-5


def shape_constants():
    p = np.arange(P)
    ti = p // NB
    before = ti[:, None] < ti[None, :]
    mask = np.where(before, DECAY ** (-1.0 - ti[:, None]) / NB, 0.0).astype(np.float32)
    mask = np.broadcast_to(mask, (P, P))
    qdecay = np.tile((DECAY ** ti)[None, None, :], (MEM, BC, 1)).reshape(MEM, BC * P).astype(np.float32)
    kscale = (DECAY ** (TI - 1.0 - ti) / NB).astype(np.float32)[:, None]
    ident = np.eye(P, dtype=np.float32)
    tri = (p[:, None] < p[None, :]).astype(np.float32)
    eye8 = np.broadcast_to(np.arange(NE, dtype=np.float32), (P, NE))
    small = np.concatenate([eye8, eye8 * REG, kscale, p.astype(np.float32)[:, None],
                            np.repeat(p[:, None], NE, axis=1), np.repeat(p[:, None] + P, NE, axis=1)], axis=1)
    square = np.concatenate([ident, mask, tri, np.ones((P, P), np.float32)], axis=1)
    chunk = np.arange(NCH)
    dest = (np.arange(2)[None, :, None] * NTOK + chunk[None, None, :] * P + p[:, None, None]).astype(np.int32)
    return {
        "c_square": np.ascontiguousarray(square),
        "c_qdecay": np.ascontiguousarray(qdecay),
        "c_small": np.ascontiguousarray(small.astype(np.float32)),
        "c_dest": np.ascontiguousarray(dest.reshape(P, 2 * NCH)),
    }


class Step:

    def __init__(self, turn, place, unroll):
        self.turn, self.place, self.unroll = turn + place // unroll, place % unroll, unroll

    def back(self, k):
        return Step(self.turn, self.place - k, self.unroll)

    @property
    def n(self):
        return self.turn * self.unroll + self.place

    def exists(self, count):
        return not isinstance(self.turn, int) or 0 <= self.n < count


def at_least(engine, sem, value):
    if not isinstance(value, int) or value > 0:
        engine.wait_ge(sem, value)


def settle(engine):
    engine.nop(nofuse=True)


def run_steps(engine, count, unroll, body):
    for place in range(unroll):
        body(Step(0, place, unroll))
    with engine.Fori(1, count // unroll) as turn:
        for place in range(unroll):
            body(Step(turn, place, unroll))


def straight(count, unroll, body, behind={}):
    for n in range(count):
        body(Step(n // unroll, n % unroll, unroll))
        if n in behind:
            behind[n]()


def build(nc, x, Wq, Wk, Wv, Wo, gate, M0, Wg, bg, W1, b1, W2, b2, c, wmod,
          c_square, c_qdecay, c_small, c_dest, out, routed, y_rows, bias_rows):
    with ExitStack() as ctx:
        def sb(name, shape, dt=F32):
            return ctx.enter_context(nc.sbuf_tensor(name, shape, dt))

        def sem(name):
            return ctx.enter_context(nc.semaphore(name))

        bank = [ctx.enter_context(nc.psum_tensor(f"bank{i}", [P, 512], F32)) for i in range(8)]

        X = sb("X", [P, NCH, D])
        W1h = sb("W1h", [P, NE * DFF], F32R)
        W1l = sb("W1l", [P, NE * DFF], F32R)
        W2hl = sb("W2hl", [P, NE * FB, 2 * D], F32R)
        B1 = sb("B1", [P, NE * DFF], F32R)
        B2 = sb("B2", [P, NE * D], F32R)
        onesR = sb("onesR", [P, P], F32R)
        square = sb("square", [P, 4 * P])
        ident = square[:, 0:P]
        small = sb("small", [P, 4 * NE + 2])
        expert_id, expert_base = small[:, 0:NE], small[:, NE:2 * NE]
        kscale, pid = small[:, 2 * NE:2 * NE + 1], small[:, 2 * NE + 1:2 * NE + 2]
        tile_id = small[:, 2 * NE + 2:].rearrange("p (h e) -> p h e", h=2)
        qdecay = sb("qdecay", [MEM, BC * P])
        dest = sb("dest", [P, 2, NCH], I32)
        tri = sb("tri", [P, P], BF16)
        ones = sb("ones", [P, P], BF16)
        mod = sb("mod", [P, 6, D])
        wqk = sb("wqk", [P, 2 * MEM])
        wvo = sb("wvo", [P, D])
        WgS = sb("WgS", [P, NE])
        bgS = sb("bgS", [P, NE])
        top = sb("top", [P, NCH, 8])
        pairw = sb("pairw", [P, 2, NCH])
        stage = sb("stage", [P, 2, HALF])
        cS = sb("cS", [NB, 3, D])
        scT = sb("scT", [P, P])
        wsm = sb("wsm", [P, 3 * D + MEM + 1])
        woT = sb("woT", [MEM, D])
        M0S = sb("M0S", [MEM, MEM])
        bS = sb("bS", [P, MEM + NE])
        bH = sb("bH", [P, MEM + NE], F32R)
        bL = sb("bL", [P, MEM + NE], F32R)
        hn = sb("hn", [P, 2, BC, D])
        wmS = hn[:].rearrange("p a c d -> p (a c d)")[:, 0:6 * D]
        hT = sb("hT", [P, BC * P])
        qT = sb("qT", [MEM, 2, BC * P])
        kT = sb("kT", [MEM, 2, BC * P])
        vS = sb("vS", [P, 2, BC, D])
        kS = sb("kS", [P, 2, BC, MEM])
        aS = sb("aS", [P, BC, P])
        att = sb("att", [P, BC, D])
        Mst = sb("Mst", [MEM, 2, BC, D])
        st6 = sb("st6", [P, 2 * BC, 6])
        mv = sb("mv", [P, 2 * BC, 2])
        rs = sb("rs", [P, 5, 2 * BC])
        rows = sb("rows", [P, RB, 2, BC, ROWW])
        h2T = sb("h2T", [P, BC * P])
        lg = sb("lg", [P, BC, NE])
        rs8 = sb("sorted8", [P, BC, 8])
        chosen = sb("chosen", [P, BC, 8], U32)
        chosen_f = sb("chosen_f", [P, BC, 8])
        oh = sb("oh", [P, 2, BC, NE])
        T = sb("T", [P, BC, NE], BF16)
        cum = sb("cum", [P, 2, NE])
        cumb = sb("cumb", [P, NE], BF16)
        rk = sb("rk", [P, BC, NE])
        rk2 = sb("rk2", [P, 2, BC, NE])
        posf = sb("posf", [P, 2 * BC])
        pos = sb("pos", [P, RB, 2 * BC], I32)
        padrow = sb("padrow", [P, ROWW])
        padpos = sb("padpos", [P, NE + 1], I32)
        padf = sb("padf", [P, NE + 1])
        cnt_i = sb("cnt_i", [P, NE], I32)
        tiles_f = sb("tiles_f", [P, 3, NE])
        beyond = sb("beyond", [P, 2, 2, NE])
        tab = sb("tab", [P, 3, 2])
        tile_row = sb("tile_row", [1, NTILE], I32)
        tile_exp = sb("tile_exp", [1, NTILE], I32)
        tin = rows[:, 0].rearrange("p k c w -> p (k c) w")
        th = sb("th", [P, 2, P], F32R)
        tl = sb("tl", [P, 2, P], F32R)
        g = stage[:, 0, 0:2 * DFF].rearrange("p (b f) -> p b f", b=2)
        gh = sb("gh", [P, 2, DFF], F32R)
        gl = sb("gl", [P, 2, DFF], F32R)
        ysb = hn[:].rearrange("p a c d -> p (a c) d")
        yb = stage[:, 1, :].rearrange("p (b k c d) -> p b k c d", b=2, k=2, c=BC)[:, :, :, :, :]

        S = {n: sem(n) for n in (
            "consts_in", "wmod_in", "w1_in0", "w1_in1", "w2_in0", "w2_in1", "biases_split", "biases_out", "biases_in", "act_setup",
            "silu_ready", "transposed", "copied", "products", "setup_done", "split_hi", "split_lo", "zeroed",
            "ln_var", "ln_sd", "ln_ready", "z1", "z2", "h_ready", "hT_ps", "hT_ready", "qk_ps", "v_ps",
            "q_ready", "k_ready", "v_ready", "s_ps", "a_ready", "u_ps", "m_ready", "o_ps", "o_read",
            "h2_ready", "h2_copied", "dest_set", "h2T_ps", "h2T_ready", "lg_ps", "t_ready", "rk_ps", "pos_ready",
            "dve", "cum_ready", "cnt_ps", "tab_cols", "tab_ps", "pads_ready", "pads_in", "table_ready",
            "exp_in", "exp_ready", "w_ready",
            "th_ps", "th_ready", "mm1", "gelu", "gt_ps", "gh_ready", "gl_ready", "y_ps", "y_ready",
            "y0_scaled", "y_weighted", "y_summed", "sum_ready", "out_done",
        )}
        x_in = [sem(f"x_in{i}") for i in range(2)]
        rows_out = [sem(f"rows_out{i}") for i in range(RB)]
        tile_in = [sem(f"tile_in{i}") for i in range(SLOTS)]
        tile_out = [sem(f"tile_out{i}") for i in range(SLOTS)]
        y_in = [sem(f"y_in{i}") for i in range(2)]

        x_v = x.rearrange("b (n c t) d -> n t b c d", c=BC, t=TI)
        out_v = out.rearrange("b (n c t) d -> n t b c d", c=BC, t=TI)
        y_v = y_rows.rearrange("(k n c p) d -> k n p c d", k=2, p=P, c=BC)

        def chunk(n, j):
            return X[:, bass.ds(n.n * BC + j, 1), :].rearrange("p a d -> p (a d)")

        def group(n):
            return X[:, bass.ds(n.n * BC, BC), :]

        loads = ((square[:], c_square), (small[:], c_small), (cS[:, 0, :], c), (WgS[:], Wg), (M0S[:], M0),
                 (bgS[:], bg.rearrange("(a e) -> a e", a=1).broadcast_to((P, NE))),
                 (wsm[0:MEM, 0:D], Wq), (wsm[0:MEM, D:2 * D], Wk), (wsm[0:MEM, 2 * D:3 * D], Wv),
                 (wsm[:, 3 * D:3 * D + MEM], Wo),
                 (wsm[:, 3 * D + MEM:], gate.rearrange("(a e) -> a e", a=1).broadcast_to((P, 1))),
                 (bS[:, 0:MEM], b1.rearrange("e (q f) -> (e q) f", f=MEM)),
                 (bS[:, MEM:], b2.rearrange("e (q f) -> (e q) f", f=NE)),
                 (qdecay[:], c_qdecay), (dest[:].rearrange("p k c -> p (k c)"), c_dest))
        CONSTS = 16 * len(loads)

        def has(n):
            return 0 <= n < NG

        def norm_columns(n):
            return slice(0 if has(n) else BC, 2 * BC if has(n - 2) else BC)

        def rows_sent(buffer, groups):
            return 16 * 2 * BC * len(range(buffer, groups, RB))

        block = ctx.enter_context(nc.Block())

        @block.sync
        def _(sp):
            for dst, src in loads:
                sp.dma_start(dst, src).then_inc(S["consts_in"], 16)
            sp.dma_start(wmS, wmod).then_inc(S["wmod_in"], 16)

            def load_x(n):
                at_least(sp, S["hT_ps"], n.n - 1)
                settle(sp)
                for t in range(TI):
                    sp.dma_start(X[t * NB:(t + 1) * NB, bass.ds(n.n * BC, BC), :], x_v[n.n, t]).then_inc(
                        x_in[n.place], 16)

            load_x(Step(0, 0, 2))
            load_x(Step(0, 1, 2))
            HE = NE // 2
            w1_v, w2_v = W1.rearrange("e d f -> d e f"), W2.rearrange("e (f p) d -> p e f d", p=P)
            for i in range(2):
                sp.dma_start(stage[:, i, :].rearrange("p (e f) -> p e f", e=HE),
                             w1_v[:, i * HE:(i + 1) * HE]).then_inc(S[f"w1_in{i}"], 16)
            sp.wait_ge(S["biases_split"], 2)
            for i, part in enumerate((bH, bL)):
                sp.dma_start(bias_rows[i, 0:NE * DFF].rearrange("(p f) -> p f", p=P),
                             part[:, 0:MEM].bitcast(F32)).then_inc(S["biases_out"], 16)
                sp.dma_start(bias_rows[i, NE * DFF:].rearrange("(p f) -> p f", p=P),
                             part[:, MEM:].bitcast(F32)).then_inc(S["biases_out"], 16)
            for i in range(2):
                sp.wait_ge(S["split_lo"], i + 1)
                sp.dma_start(stage[:, i, :].rearrange("p (e f d) -> p e f d", e=HE, f=FB),
                             w2_v[:, i * HE:(i + 1) * HE]).then_inc(S[f"w2_in{i}"], 16)
            with sp.Fori(1, NG // 2) as turn:
                load_x(Step(turn, 0, 2))
                load_x(Step(turn, 1, 2))
            sp.wait_ge(S["biases_out"], 64)
            sp.wait_ge(S["zeroed"], 3)
            for i in range(2):
                sp.dma_start(B1[32 * i:32 * i + 1, :].bitcast(F32),
                             bias_rows[i:i + 1, 0:NE * DFF]).then_inc(S["biases_in"], 16)
                sp.dma_start(B2[32 * i:32 * i + 1, :].bitcast(F32),
                             bias_rows[i:i + 1, NE * DFF:]).then_inc(S["biases_in"], 16)

            sp.wait_ge(S["table_ready"], 2)
            sp.wait_ge(S["pads_in"], 16 * (NE + 1))
            for s in range(RB):
                sp.wait_ge(rows_out[s], rows_sent(s, NG))

            def load_tile(j):
                at_least(sp, S["th_ps"], j.n - SLOTS + 1)
                settle(sp)
                at_least(sp, tile_out[j.place], j.turn * 16)
                settle(sp)
                row = sp.value_load(tile_row[0:1, bass.ds(j.n, 1)], min_val=0, max_val=PAD_ROW)
                sp.dma_start(tin[:, j.place, :], routed[bass.ds(row, P), :]).then_inc(tile_in[j.place], 16)
            run_steps(sp, NTILE, SLOTS, load_tile)

            for s in range(SLOTS):
                sp.wait_ge(tile_out[s], 16 * NTILE // SLOTS)

            def load_y(n):
                at_least(sp, S["sum_ready"], n.n - 1)
                settle(sp)
                for k in range(2):
                    sp.dma_start(yb[:, n.place, k], y_v[k, n.n]).then_inc(y_in[n.place], 16)
            run_steps(sp, NG, 2, load_y)

        @block.gpsimd
        def _(pool):
            pool.memset(B1[:].bitcast(F32), 0.0).then_inc(S["zeroed"], 1)
            pool.memset(B2[:].bitcast(F32), 0.0).then_inc(S["zeroed"], 1)
            pool.memset(padrow[:, 0:D], 0.0).then_inc(S["zeroed"], 1)
            pool.memset(padrow[:, D:].bitcast(I32), SKIP).then_inc(S["zeroed"], 1)
            pool.memset(rows[:, :, :, :, D + 1:], 0.0).then_inc(S["zeroed"], 1)
            for i in range(2):
                pool.wait_ge(S["split_hi"], i + 1)
                cols = slice(i * HALF, (i + 1) * HALF)
                pool.tensor_tensor(W1l[:, cols], stage[:, i, :], W1h[:, cols].bitcast(F32), ALU.subtract).then_inc(
                    S["split_lo"], 1)
            for i in range(2):
                pool.wait_ge(S["split_hi"], i + 3)
                part = W2hl[:, i * NE * FB // 2:(i + 1) * NE * FB // 2, :]
                pool.tensor_tensor(part[:, :, D:2 * D], stage[:, i, :].rearrange("p (e d) -> p e d", d=D),
                                   part[:, :, 0:D].bitcast(F32), ALU.subtract).then_inc(S["split_lo"], 1)

            for n in range(NG):
                pool.wait_ge(S["pos_ready"], n + 1)
                pool.wait_ge(S["dest_set"], n + 1)
                pool.wait_ge(S["h2_ready"], n + 1)
                pool.wait_ge(S["h2_copied"], n + 1)
                for k in range(2):
                    for j in range(BC):
                        pool.indirect_dma_start(
                            routed, bass.IndirectOffsetOnAxis(pos[:, n % RB, k * BC + j:k * BC + j + 1], 0),
                            rows[:, n % RB, k, j, :], None).then_inc(rows_out[n % RB], 16)

            pool.wait_ge(S["pads_ready"], 1)
            for e in range(NE + 1):
                pool.indirect_dma_start(
                    routed, bass.IndirectOffsetOnAxis(padpos[:, e:e + 1], 0), padrow[:], None).then_inc(
                        S["pads_in"], 16)

            def put_y(j):
                pool.wait_ge(S["y_ready"], j.n + 1)
                settle(pool)
                pool.indirect_dma_start(
                    y_rows, bass.IndirectOffsetOnAxis(tin[:, j.place, D:D + 1].bitcast(I32), 0),
                    ysb[:, j.place, :], None, bounds_check=2 * NTOK - 1, oob_is_err=False).then_inc(
                        tile_out[j.place], 16)
            run_steps(pool, NTILE, SLOTS, put_y)

            def add_x(n):
                pool.wait_ge(S["y_summed"], n.n + 1)
                settle(pool)
                pool.tensor_tensor(group(n), group(n), yb[:, n.place, 0], ALU.add).then_inc(S["sum_ready"], 1)
            run_steps(pool, NG, 2, add_x)

        @block.scalar
        def _(act):
            act.wait_ge(S["consts_in"], CONSTS)
            act.activation(cS[:, 1, :], cS[:, 0, :], ACT.Exp, scale=-1.0).then_inc(S["act_setup"], 1)
            act.activation(wsm[:, 3 * D + MEM:], wsm[:, 3 * D + MEM:], ACT.Exp, scale=-1.0).then_inc(
                S["act_setup"], 1)

            def norm_roots(n):
                at = norm_columns(n)
                act.wait_ge(S["ln_var"], n + 1)
                act.activation(rs[:, 1, at], rs[:, 0, at], ACT.Sqrt).then_inc(S["ln_sd"], 1)

            def normalize(n, half, dst, done):
                for j in range(BC):
                    i = half * BC + j
                    ins = act.activation(dst[:, j, :], X[:, n * BC + j, :], ACT.Identity, scale=rs[:, 2, i:i + 1],
                                         bias=rs[:, 4, i:i + 1])
                ins.then_inc(S[done], 1)

            def steps(n):
                f, m, l = n, n - 2, n - 3
                if has(l):
                    act.wait_ge(S["h2T_ps"], l + 1)
                    at_least(act, S["lg_ps"], l)
                    act.activation(h2T[:], bank[0][:], ACT.Copy).then_inc(S["h2T_ready"], 1)
                if has(f) or has(m):
                    norm_roots(n)
                    act.wait_ge(S["ln_ready"], n + 1)
                if has(f):
                    at_least(act, S["hT_ps"], f - 1)
                    normalize(f, 0, hn[:, f % 2], "z1")
                if has(m):
                    at_least(act, rows_out[m % RB], rows_sent(m % RB, m))
                    at_least(act, S["h2T_ps"], m - RB + 1)
                    normalize(m, 1, rows[:, m % RB, 0, :, 0:D], "z2")
                if has(f):
                    act.wait_ge(S["hT_ps"], f + 1)
                    at_least(act, S["v_ps"], f)
                    act.activation(hT[:], bank[0][:], ACT.Copy).then_inc(S["hT_ready"], 1)
                if has(m):
                    act.wait_ge(S["h2_ready"], m + 1)
                    act.activation(rows[:, m % RB, 1, :, 0:D], rows[:, m % RB, 0, :, 0:D], ACT.Copy).then_inc(
                        S["h2_copied"], 1)
                if has(f):
                    b = f % 2
                    act.wait_ge(S["qk_ps"], f + 1)
                    at_least(act, S["o_ps"], f - 1)
                    q = bank[1][0:MEM, :].rearrange("p (c t b) -> p c t b", c=BC, t=TI)
                    for t in range(TI):
                        ins = act.activation(qT[:, b].rearrange("p (c t b) -> p c t b", c=BC, t=TI)[:, :, t, :],
                                             q[:, :, t, :], ACT.Copy, scale=DECAY ** t)
                    ins.then_inc(S["q_ready"], 1)
                    act.activation(kT[:, b, :], bank[1][MEM:2 * MEM, :], ACT.Copy).then_inc(S["k_ready"], 1)
                    act.wait_ge(S["v_ps"], f + 1)
                    act.activation(vS[:, b], bank[3][:].rearrange("p (c d) -> p c d", c=BC), ACT.Copy).then_inc(
                        S["v_ready"], 1)
                    act.activation(kS[:, b], bank[2][:, 0:BC * MEM].rearrange("p (c d) -> p c d", c=BC),
                                   ACT.Copy, scale=kscale).then_inc(S["v_ready"], 1)

            def split_w1():
                for i in range(2):
                    act.wait_ge(S[f"w1_in{i}"], 16)
                    act.activation(W1h[:, i * HALF:(i + 1) * HALF], stage[:, i, :], ACT.Copy).then_inc(
                        S["split_hi"], 1)

            def split_w2():
                for i in range(2):
                    act.wait_ge(S[f"w2_in{i}"], 16)
                    act.activation(W2hl[:, i * NE * FB // 2:(i + 1) * NE * FB // 2, 0:D],
                                   stage[:, i, :].rearrange("p (e d) -> p e d", d=D), ACT.Copy).then_inc(
                                       S["split_hi"], 1)

            for n in range(NG + 3):
                steps(n)
                if n == 0:
                    split_w1()
                if n == 1:
                    split_w2()
            act.wait_ge(S["exp_in"], 1)
            act.activation(pairw[:, 1, :], pairw[:, 0, :], ACT.Exp).then_inc(S["exp_ready"], 1)

            def tile(n):
                j = n.back(1)
                if j.exists(NTILE):
                    act.wait_ge(S["mm1"], j.n + 1)
                    at_least(act, S["gt_ps"], j.n - 1)
                    act.activation(g[:, j.place % 2, :], bank[2 + j.place % 2][:], ACT.Gelu).then_inc(S["gelu"], 1)
                j = n.back(2)
                if j.exists(NTILE):
                    act.wait_ge(S["gt_ps"], j.n + 1)
                    at_least(act, S["y_ps"], j.n - 1)
                    act.activation(gh[:, j.place % 2, :], bank[4 + j.place % 2][:], ACT.Copy).then_inc(
                        S["gh_ready"], 1)
            act.wait_ge(S["split_lo"], 4)
            straight(NTILE + 2, SLOTS, tile)

            def end(n):
                if n.exists(NG):
                    act.wait_ge(y_in[n.place], (n.turn + 1) * 32)
                    for j in range(BC):
                        ins = act.activation(yb[:, n.place, 0, j, :], yb[:, n.place, 0, j, :], ACT.Copy,
                                             scale=pairw[:, 0, bass.ds(n.n * BC + j, 1)])
                    ins.then_inc(S["y0_scaled"], 1)
                m = n.back(1)
                if m.exists(NG):
                    act.wait_ge(S["sum_ready"], m.n + 1)
                    for t in range(TI):
                        act.dma_start(out_v[m.n, t], X[t * NB:(t + 1) * NB, bass.ds(m.n * BC, BC), :]).then_inc(
                            S["out_done"], 16)
            act.wait_ge(S["w_ready"], 1)
            straight(NG + 1, 2, end)
            act.wait_ge(S["out_done"], 16 * TI * NG)

        @block.vector
        def _(dve):
            chain = [0]

            def mark(ins):
                chain[0] += 1
                ins.then_inc(S["dve"], 1)

            def then(ins):
                mark(ins)
                dve.wait_ge(S["dve"], chain[0])

            dve.wait_ge(S["consts_in"], CONSTS)
            mark(dve.tensor_copy(tri[:], square[:, 2 * P:3 * P]))
            mark(dve.tensor_copy(ones[:], square[:, 3 * P:4 * P]))
            mark(dve.tensor_copy(onesR[:], square[:, 3 * P:4 * P]))
            dve.tensor_copy(bH[:], bS[:]).then_inc(S["biases_split"], 1)
            dve.wait_ge(S["biases_split"], 1)
            dve.tensor_tensor(bL[:], bS[:], bH[:].bitcast(F32), ALU.subtract).then_inc(S["biases_split"], 1)
            dve.wait_ge(S["act_setup"], 2)
            gt = wsm[:, 3 * D + MEM:]
            then(dve.tensor_scalar(cS[:, 2, :], cS[:, 1, :], 1.0, None, ALU.add))
            then(dve.reciprocal(cS[:, 1, :], cS[:, 2, :]))
            dve.tensor_tensor(cS[:, 2, :], cS[:, 1, :], cS[:, 0, :], ALU.mult).then_inc(S["silu_ready"], 1)
            then(dve.tensor_scalar(gt, gt, 1.0, None, ALU.add))
            then(dve.reciprocal(gt, gt))
            dve.wait_ge(S["transposed"], 1)
            dve.tensor_copy(scT[:].rearrange("p (t b) -> p t b", t=TI),
                            bank[0][:, 0:NB].rearrange("p (t b) -> p t b", t=1).broadcast_to(
                                (P, TI, NB))).then_inc(S["copied"], 1)
            dve.tensor_copy(wqk[:], bank[0][:, NB:NB + 2 * MEM]).then_inc(S["copied"], 1)
            dve.tensor_copy(woT[:], bank[0][0:MEM, P:P + D]).then_inc(S["copied"], 1)
            dve.wait_ge(S["products"], 1)
            then(dve.memset(cum[:], 0.0))
            mark(dve.memset(cumb[:], 0.0))
            mark(dve.tensor_copy(wvo[:], bank[2][:, 0:D]))
            mark(dve.tensor_copy(Mst[:, 0, 0, :], bank[3][0:MEM, 0:D]))
            mark(dve.tensor_copy(mod[:, 0:3, :], bank[4][:, 0:3 * D].rearrange("p (s d) -> p s d", s=3)))
            then(dve.tensor_copy(mod[:, 3:6, :], bank[5][:, 0:3 * D].rearrange("p (s d) -> p s d", s=3)))
            for i in (1, 4):
                then(dve.tensor_scalar(mod[:, i, :], mod[:, i, :], 1.0, None, ALU.add))
            for i in (2, 5):
                mark(dve.tensor_scalar(att[:, 0, :], mod[:, i, :], 0.0, 2.0, ALU.is_ge, ALU.mult))
                then(dve.tensor_scalar(att[:, 2, :], mod[:, i, :], -1.0, 0.25, ALU.mult, ALU.max))
                then(dve.tensor_tensor(att[:, 1, :], mod[:, i, :], att[:, 2, :], ALU.max))
                then(dve.scalar_tensor_tensor(out=mod[:, i, :], in0=att[:, 0, :], scalar=-1.0, in1=att[:, 1, :],
                                              op0=ALU.add, op1=ALU.mult))
            dve.tensor_scalar(mod[:, 2, :], mod[:, 2, :], gt, None, ALU.mult).then_inc(S["setup_done"], 1)
            dve.wait_ge(S["setup_done"], 1)

            def per_token(i):
                return mod[:, i:i + 1, :].broadcast_to((P, BC, D))

            def statistics(n):
                f, m = n, n - 2
                if has(f):
                    dve.wait_ge(x_in[f % 2], (f // 2 + 1) * (TI * 16))
                    for j in range(BC):
                        mark(dve.bn_stats(st6[:, j, :], X[:, f * BC + j, :]))
                if has(m):
                    for j in range(BC):
                        mark(dve.bn_stats(st6[:, BC + j, :], X[:, m * BC + j, :]))
                at = norm_columns(n)
                dve.wait_ge(S["dve"], chain[0])
                for i in range(at.start, at.stop):
                    mark(dve.bn_aggr(mv[:, i, :], st6[:, i, :]))
                dve.wait_ge(S["dve"], chain[0])
                at_least(dve, S["z1"], min(n, NG))
                at_least(dve, S["z2"], n - 2)
                dve.tensor_scalar(rs[:, 0, at], mv[:, at, 1], EPS, None, ALU.add).then_inc(S["ln_var"], 1)

            def roots(n):
                at = norm_columns(n)
                v, sd, r, t, nb = (rs[:, i, at] for i in range(5))
                dve.wait_ge(S["ln_sd"], n + 1)
                then(dve.reciprocal(r, sd))
                then(dve.tensor_tensor(t, r, r, ALU.mult))
                then(dve.tensor_tensor(t, t, v, ALU.mult))
                then(dve.tensor_scalar(t, t, -0.5, 1.5, ALU.mult, ALU.add))
                then(dve.tensor_tensor(r, r, t, ALU.mult))
                dve.scalar_tensor_tensor(out=nb, in0=mv[:, at, 0], scalar=-1.0, in1=r, op0=ALU.mult,
                                         op1=ALU.mult).then_inc(S["ln_ready"], 1)

            def modulate(n):
                f, m = n, n - 2
                z1, z2 = hn[:, f % 2], rows[:, m % RB, 0, :, 0:D]
                if has(f):
                    dve.wait_ge(S["z1"], f + 1)
                    mark(dve.tensor_tensor(z1, z1, per_token(1), ALU.mult))
                    c1 = chain[0]
                if has(m):
                    dve.wait_ge(S["z2"], m + 1)
                    mark(dve.tensor_tensor(z2, z2, per_token(4), ALU.mult))
                    c2 = chain[0]
                if has(f):
                    dve.wait_ge(S["dve"], c1)
                    dve.tensor_tensor(z1, z1, per_token(0), ALU.add).then_inc(S["h_ready"], 1)
                if has(m):
                    dve.wait_ge(S["dve"], c2)
                    dve.tensor_tensor(z2, z2, per_token(3), ALU.add).then_inc(S["h2_ready"], 1)

            def scores(n):
                dve.wait_ge(S["s_ps"], n + 1)
                at_least(dve, S["o_ps"], n)
                dve.tensor_tensor(aS[:], bank[4][:].rearrange("p (c t) -> p c t", c=BC),
                                  square[:, P:2 * P].rearrange("p (a t) -> p a t", a=1).broadcast_to((P, BC, P)),
                                  ALU.mult).then_inc(S["a_ready"], 1)

            def states(n):
                dve.wait_ge(S["u_ps"], n + 1)
                for j in range(BC):
                    to = Mst[:, n % 2, j + 1, :] if j < BC - 1 else Mst[:, 1 - n % 2, 0, :]
                    dve.scalar_tensor_tensor(out=to, in0=Mst[:, n % 2, j, :], scalar=DECAY ** TI,
                                             in1=bank[5][0:MEM, j * D:(j + 1) * D], op0=ALU.mult,
                                             op1=ALU.add).then_inc(S["m_ready"], 1)
                    dve.wait_ge(S["m_ready"], n * BC + j + 1)

            def residual(n):
                dve.wait_ge(S["o_ps"], n + 1)
                dve.tensor_tensor(att[:], bank[7][:].rearrange("p (c d) -> p c d", c=BC), per_token(2),
                                  ALU.mult).then_inc(S["o_read"], 1)
                dve.wait_ge(S["o_read"], n + 1)
                xs = X[:, n * BC:(n + 1) * BC, :]
                then(dve.tensor_tensor(xs, xs, att[:], ALU.add))

            def destinations(n):
                at_least(dve, rows_out[n % RB], rows_sent(n % RB, n))
                for k in range(2):
                    ins = dve.tensor_copy(rows[:, n % RB, k, :, D:D + 1].bitcast(I32).rearrange("p c a -> p (c a)"),
                                          dest[:, k, n * BC:(n + 1) * BC])
                ins.then_inc(S["dest_set"], 1)

            def choose(n):
                dve.wait_ge(S["lg_ps"], n + 1)
                then(dve.tensor_tensor(lg[:], bank[6][:, 0:BC * NE].rearrange("p (c e) -> p c e", c=BC),
                                       bgS[:].rearrange("p (a e) -> p a e", a=1).broadcast_to((P, BC, NE)), ALU.add))
                tops = [rs8[:, j, :] for j in range(BC)]
                for j in range(BC):
                    mark(dve.max(tops[j], lg[:, j, :]))
                dve.wait_ge(S["dve"], chain[0])
                for j in range(BC):
                    mark(dve.max_index(chosen[:, j, :], tops[j], lg[:, j, :]))
                mark(dve.tensor_copy(top[:, n * BC:(n + 1) * BC, :], rs8[:]))
                dve.wait_ge(S["dve"], chain[0])
                then(dve.tensor_copy(chosen_f[:], chosen[:]))
                for k in range(2):
                    mark(dve.tensor_tensor(oh[:, k], chosen_f[:, :, k:k + 1].broadcast_to((P, BC, NE)),
                                           expert_id.rearrange("p (a e) -> p a e", a=1).broadcast_to((P, BC, NE)),
                                           ALU.is_equal))
                dve.wait_ge(S["dve"], chain[0])
                dve.tensor_tensor(T[:], oh[:, 0], oh[:, 1], ALU.add).then_inc(S["t_ready"], 1)

            def place(n):
                dve.wait_ge(S["rk_ps"], n + 1)
                mark(dve.tensor_reduce(cum[:, 1, :], T[:].rearrange("p c e -> p e c"), AX_X, ALU.add))
                then(dve.tensor_tensor(rk[:], bank[6][:, P:P + BC * NE].rearrange("p (c e) -> p c e", c=BC),
                                       expert_base.rearrange("p (a e) -> p a e", a=1).broadcast_to((P, BC, NE)),
                                       ALU.add))
                mark(dve.tensor_tensor(cum[:, 0, :], cum[:, 0, :], cum[:, 1, :], ALU.add))
                for k in range(2):
                    mark(dve.tensor_tensor(rk2[:, k], rk[:], oh[:, k], ALU.mult))
                dve.wait_ge(S["dve"], chain[0])
                dve.tensor_copy(cumb[:], cum[:, 0, :]).then_inc(S["cum_ready"], 1)
                then(dve.tensor_reduce(posf[:], rk2[:].rearrange("p k c e -> p (k c) e"), AX_X, ALU.add))
                at_least(dve, rows_out[n % RB], rows_sent(n % RB, n))
                dve.tensor_copy(pos[:, n % RB, :], posf[:]).then_inc(S["pos_ready"], 1)

            def steps(n):
                if has(n - 2):
                    residual(n - 2)
                if has(n) or has(n - 2):
                    statistics(n)
                if has(n - 1):
                    scores(n - 1)
                    states(n - 1)
                if has(n) or has(n - 2):
                    roots(n)
                if has(n - 2):
                    destinations(n - 2)
                if has(n - 3):
                    choose(n - 3)
                if has(n) or has(n - 2):
                    modulate(n)
                if has(n - 3):
                    place(n - 3)
            for n in range(NG + 3):
                steps(n)

            dve.wait_ge(S["cnt_ps"], 1)
            cnt = bank[6][:, 2 * P:2 * P + NE]
            mark(dve.memset(padf[:, NE:NE + 1], float(PAD_ROW)))
            then(dve.tensor_tensor(padf[:, 0:NE], cnt, expert_base, ALU.add))
            mark(dve.tensor_scalar(cnt_i[:], cnt, float(P - 1), None, ALU.add))
            then(dve.tensor_scalar(padf[:], padf[:], pid, None, ALU.add))
            dve.wait_ge(S["zeroed"], 5)
            dve.tensor_copy(padpos[:], padf[:]).then_inc(S["pads_ready"], 1)
            tiles, upto, jump = tiles_f[:, 0, :], tiles_f[:, 1, :], tiles_f[:, 2, :]
            then(dve.tensor_scalar(cnt_i[:], cnt_i[:], 7, None, ALU.logical_shift_right))
            then(dve.tensor_copy(tiles, cnt_i[:]))
            mark(dve.tensor_scalar(jump, tiles, float(-P), float(REG), ALU.mult, ALU.add))
            then(dve.tensor_tensor_scan(upto, square[:, 3 * P:3 * P + NE], tiles, 0.0, ALU.mult, ALU.add))
            then(dve.tensor_tensor(beyond[:, 0], tile_id, upto.rearrange("p (a e) -> p a e", a=1).broadcast_to(
                (P, 2, NE)), ALU.is_ge))
            then(dve.tensor_tensor(beyond[:, 1], beyond[:, 0], jump.rearrange("p (a e) -> p a e", a=1).broadcast_to(
                (P, 2, NE)), ALU.mult))
            mark(dve.tensor_reduce(tab[:, 0, :], beyond[:, 0], AX_X, ALU.add))
            then(dve.tensor_reduce(tab[:, 1, :], beyond[:, 1], AX_X, ALU.add))
            mark(dve.tensor_scalar(tab[:, 0, :], tab[:, 0, :], float(NE - 1), None, ALU.min))
            then(dve.scalar_tensor_tensor(out=tab[:, 1, :], in0=tile_id[:, :, 0], scalar=float(P), in1=tab[:, 1, :],
                                          op0=ALU.mult, op1=ALU.add))
            dve.tensor_scalar(tab[:, 1, :], tab[:, 1, :], float(PAD_ROW), None, ALU.min).then_inc(S["tab_cols"], 1)
            dve.tensor_tensor(pairw[:, 0, :], top[:, :, 1], top[:, :, 0], ALU.subtract).then_inc(S["exp_in"], 1)
            dve.wait_ge(S["tab_ps"], 1)
            dve.tensor_copy(tile_exp[:], bank[0][0:1, 0:NTILE]).then_inc(S["table_ready"], 1)
            dve.tensor_copy(tile_row[:], bank[0][0:1, 2 * P:2 * P + NTILE]).then_inc(S["table_ready"], 1)
            dve.wait_ge(S["exp_ready"], 1)
            then(dve.tensor_scalar(pairw[:, 0, :], pairw[:, 1, :], 1.0, None, ALU.add))
            then(dve.reciprocal(pairw[:, 0, :], pairw[:, 0, :]))
            dve.tensor_tensor(pairw[:, 1, :], pairw[:, 1, :], pairw[:, 0, :], ALU.mult).then_inc(S["w_ready"], 1)

            def tile(n):
                j, b = n, n.place % 2
                if j.exists(NTILE):
                    dve.wait_ge(S["th_ps"], j.n + 1)
                    at_least(dve, S["mm1"], j.n - 1)
                    dve.tensor_copy(th[:, b, :], bank[b][:, 0:P]).then_inc(S["th_ready"], 1)
                    dve.wait_ge(S["th_ready"], j.n * 2 + 1)
                    dve.tensor_tensor(tl[:, b, :], bank[b][:, 0:P], th[:, b, :].bitcast(F32),
                                      ALU.subtract).then_inc(S["th_ready"], 1)
                j = n.back(3)
                b = j.place % 2
                if j.exists(NTILE):
                    dve.wait_ge(S["y_ps"], j.n + 1)
                    at_least(dve, tile_out[j.place], j.turn * 16)
                    dve.tensor_reduce(ysb[:, j.place, :],
                                      bank[6 + b][:, 0:2 * D].rearrange("p (h d) -> p d h", h=2), AX_X,
                                      ALU.add).then_inc(S["y_ready"], 1)
                j = n.back(2)
                b = j.place % 2
                if j.exists(NTILE):
                    dve.wait_ge(S["gh_ready"], j.n + 1)
                    at_least(dve, S["y_ps"], j.n - 1)
                    dve.tensor_tensor(gl[:, b, :], bank[4 + b][:], gh[:, b, :].bitcast(F32),
                                      ALU.subtract).then_inc(S["gl_ready"], 1)
            straight(NTILE + 3, SLOTS, tile)

            def end(n):
                dve.wait_ge(S["y0_scaled"], n.n + 1)
                for j in range(BC):
                    ins = dve.scalar_tensor_tensor(
                        out=yb[:, n.place, 0, j, :], in0=yb[:, n.place, 1, j, :],
                        scalar=pairw[:, 1, bass.ds(n.n * BC + j, 1)], in1=yb[:, n.place, 0, j, :],
                        op0=ALU.mult, op1=ALU.add)
                ins.then_inc(S["y_weighted"], 1)
                dve.wait_ge(S["y_weighted"], n.n + 1)
                dve.tensor_tensor(yb[:, n.place, 0], yb[:, n.place, 0], per_token(5), ALU.mult).then_inc(
                    S["y_summed"], 1)
            dve.wait_ge(S["w_ready"], 1)
            straight(NG, 2, end)

        @block.tensor
        def _(pe):
            pe.wait_ge(S["consts_in"], CONSTS)
            pe.transpose(bank[0][:, NB:NB + MEM], wsm[0:MEM, 0:D], ident[0:MEM, 0:MEM])
            pe.transpose(bank[0][:, NB + MEM:NB + 2 * MEM], wsm[0:MEM, D:2 * D], ident[0:MEM, 0:MEM])
            pe.transpose(bank[0][0:MEM, P:P + D], wsm[:, 3 * D:3 * D + MEM], ident)
            pe.wait_ge(S["silu_ready"], 1)
            pe.transpose(bank[0][:, 0:NB], cS[:, 2, :], ident[0:NB, 0:NB]).then_inc(S["transposed"], 1)
            pe.wait_ge(S["copied"], 3)
            pe.wait_ge(S["wmod_in"], 16)
            pe.matmul(bank[2][:, 0:D], wsm[0:MEM, 2 * D:3 * D], woT[:], start=True, stop=True)
            pe.matmul(bank[3][0:MEM, 0:D], M0S[:], woT[:], start=True, stop=True)
            pe.matmul(bank[4][:, 0:3 * D], scT[:], wmS[:, 0:3 * D], start=True, stop=True)
            pe.matmul(bank[5][:, 0:3 * D], scT[:], wmS[:, 3 * D:6 * D], start=True, stop=True).then_inc(
                S["products"], 1)
            pe.wait_ge(S["setup_done"], 1)

            def front(n):
                pe.wait_ge(S["h_ready"], n + 1)
                at_least(pe, S["hT_ready"], n)
                at_least(pe, S["h2T_ready"], n - 2)
                for j in range(BC):
                    ins = pe.transpose(bank[0][:, j * P:(j + 1) * P], hn[:, n % 2, j, :], ident)
                ins.then_inc(S["hT_ps"], 1)
                pe.wait_ge(S["hT_ready"], n + 1)
                at_least(pe, S["q_ready"], n)
                at_least(pe, S["k_ready"], n)
                pe.matmul(bank[1][0:2 * MEM, :], wqk[:], hT[:], start=True, stop=True).then_inc(S["qk_ps"], 1)
                at_least(pe, S["v_ready"], n * 2)
                for j in range(BC):
                    pe.matmul(bank[2][:, j * MEM:(j + 1) * MEM], hT[:, j * P:(j + 1) * P], wqk[:, MEM:2 * MEM],
                              start=True, stop=True)
                    ins = pe.matmul(bank[3][:, j * D:(j + 1) * D], hT[:, j * P:(j + 1) * P], wvo[:],
                                    start=True, stop=True)
                ins.then_inc(S["v_ps"], 1)

            def middle(n):
                b = n % 2
                pe.wait_ge(S["q_ready"], n + 1)
                pe.wait_ge(S["k_ready"], n + 1)
                at_least(pe, S["a_ready"], n)
                for j in range(BC):
                    cols = slice(j * P, (j + 1) * P)
                    ins = pe.matmul(bank[4][:, cols], kT[:, b, cols], qT[:, b, cols], start=True, stop=True)
                ins.then_inc(S["s_ps"], 1)
                pe.wait_ge(S["v_ready"], n * 2 + 2)
                at_least(pe, S["m_ready"], n * BC)
                for j in range(BC):
                    ins = pe.matmul(bank[5][0:MEM, j * D:(j + 1) * D], kS[:, b, j, :], vS[:, b, j, :],
                                    start=True, stop=True)
                ins.then_inc(S["u_ps"], 1)

            def outputs(n):
                b = n % 2
                pe.wait_ge(S["a_ready"], n + 1)
                at_least(pe, S["o_read"], n)
                pe.wait_ge(S["m_ready"], n * BC + BC - 1)
                for j in range(BC):
                    cols = slice(j * P, (j + 1) * P)
                    pe.matmul(bank[7][:, cols], aS[:, j, :], vS[:, b, j, :], start=True, stop=False)
                    ins = pe.matmul(bank[7][:, cols], qT[:, b, cols], Mst[:, b, j, :], start=False, stop=True)
                ins.then_inc(S["o_ps"], 1)

            def logits(n):
                pe.wait_ge(S["h2_ready"], n + 1)
                at_least(pe, S["hT_ready"], min(n + 3, NG))
                at_least(pe, S["h2T_ready"], n)
                for j in range(BC):
                    ins = pe.transpose(bank[0][:, j * P:(j + 1) * P], rows[:, n % RB, 0, j, 0:D], ident)
                ins.then_inc(S["h2T_ps"], 1)
                pe.wait_ge(S["h2T_ready"], n + 1)
                at_least(pe, S["pos_ready"], n)
                for j in range(BC):
                    ins = pe.matmul(bank[6][:, j * NE:(j + 1) * NE], h2T[:, j * P:(j + 1) * P], WgS[:],
                                    start=True, stop=True)
                ins.then_inc(S["lg_ps"], 1)

            def ranks(n):
                pe.wait_ge(S["t_ready"], n + 1)
                at_least(pe, S["cum_ready"], n)
                r = bank[6][:, P:P + BC * NE].rearrange("p (c e) -> p c e", c=BC)
                pe.matmul(r, ones[:], cumb[:].rearrange("p (a e) -> p a e", a=1).broadcast_to((P, BC, NE)),
                          start=True, stop=False)
                for j in range(BC - 1):
                    pe.matmul(r[:, j + 1:, :], ones[:], T[:, j:j + 1, :].broadcast_to((P, BC - 1 - j, NE)),
                              start=False, stop=False)
                pe.matmul(r, tri[:], T[:], start=False, stop=True).then_inc(S["rk_ps"], 1)

            for n in range(NG + 3):
                if has(n - 1):
                    middle(n - 1)
                if has(n - 3):
                    logits(n - 3)
                if has(n - 1):
                    outputs(n - 1)
                if has(n - 3):
                    ranks(n - 3)
                if has(n):
                    front(n)

            pe.wait_ge(S["cum_ready"], NG)
            pe.matmul(bank[6][:, 2 * P:2 * P + NE], ones[:], cumb[:], start=True, stop=True).then_inc(S["cnt_ps"], 1)
            pe.wait_ge(S["tab_cols"], 1)
            for i in range(2):
                pe.matmul(bank[0][0:1, 2 * P * i:2 * P * i + P], tab[:, i, 0:1], ident, start=True, stop=True)
                ins = pe.matmul(bank[0][0:1, 2 * P * i + P:2 * P * i + NTILE], tab[:, i, 1:2],
                                ident[:, 0:NTILE - P], start=True, stop=True)
            ins.then_inc(S["tab_ps"], 1)
            pe.wait_ge(S["table_ready"], 2)
            pe.wait_ge(S["split_lo"], 4)
            pe.wait_ge(S["biases_in"], 64)

            experts = {}

            def expert(j):
                return pe.value_load(tile_exp[0:1, j.n:j.n + 1], min_val=0, max_val=NE - 1)

            def tile(n):
                j, b = n, n.place % 2
                if j.exists(NTILE):
                    pe.wait_ge(tile_in[j.place], (j.turn + 1) * 16)
                    at_least(pe, S["th_ready"], j.n * 2 - 2)
                    pe.transpose(bank[b][:, 0:P], tin[:, j.place, 0:D], ident).then_inc(S["th_ps"], 1)
                j = n.back(1)
                b = j.place % 2
                if j.exists(NTILE):
                    e = expert(j)
                    w = bass.ds(e * DFF, DFF)
                    pe.wait_ge(S["th_ready"], j.n * 2 + 2)
                    at_least(pe, S["gelu"], j.n - 1)
                    pe.matmul(bank[2 + b][:], th[:, b, :], W1h[:, w], start=True, stop=False)
                    pe.matmul(bank[2 + b][:], th[:, b, :], W1l[:, w], start=False, stop=False)
                    pe.matmul(bank[2 + b][:], tl[:, b, :], W1h[:, w], start=False, stop=False)
                    pe.matmul(bank[2 + b][:], onesR[:], B1[:, w], start=False, stop=True).then_inc(S["mm1"], 1)
                j = n.back(2)
                b = j.place % 2
                if j.exists(NTILE):
                    pe.wait_ge(S["gelu"], j.n + 1)
                    at_least(pe, S["gl_ready"], j.n - 1)
                    for f in range(FB):
                        ins = pe.transpose(bank[4 + b][:, f * P:(f + 1) * P], g[:, b, f * P:(f + 1) * P], ident)
                    ins.then_inc(S["gt_ps"], 1)
                j = n.back(3)
                b = j.place % 2
                if j.exists(NTILE):
                    e = expert(j)
                    y = bank[6 + b]
                    pe.wait_ge(S["gl_ready"], j.n + 1)
                    at_least(pe, S["y_ready"], j.n - 1)
                    for f in range(FB):
                        w2 = W2hl[:, bass.ds(e * FB + f, 1), :].rearrange("p a d -> p (a d)")
                        pe.matmul(y[:, 0:2 * D], gh[:, b, f * P:(f + 1) * P], w2, start=(f == 0), stop=False)
                        pe.matmul(y[:, 0:D], gl[:, b, f * P:(f + 1) * P], w2[:, 0:D], start=False, stop=False)
                    pe.matmul(y[:, 0:D], onesR[:], B2[:, bass.ds(e * D, D)], start=False,
                              stop=True).then_inc(S["y_ps"], 1)
            straight(NTILE + 3, SLOTS, tile)


_INS = ["L0_attn_x", "L0_attn_Wq", "L0_attn_Wk", "L0_attn_Wv", "L0_attn_Wo", "L0_attn_gate", "L0_attn_M0",
        "L0_ffn_Wg", "L0_ffn_bg", "L0_ffn_W1", "L0_ffn_b1", "L0_ffn_W2", "L0_ffn_b2", "L0_c", "L0_wmod"]


def kernel(**inputs):
    import concourse.bacc as bacc
    from concourse.bass_utils import run_bass_kernel_spmd

    nc = bacc.Bacc("TRN2", target_bir_lowering=False, num_devices=1)
    arrays = {f"in_{name}": np.ascontiguousarray(inputs[name]) for name in _INS}
    arrays.update(shape_constants())
    args = [nc.dram_tensor(name, a.shape, mybir.dt.from_np(a.dtype), kind="ExternalInput").ap()
            for name, a in arrays.items()]
    out = nc.dram_tensor("out_0", (NB, NT, D), F32, kind="ExternalOutput").ap()
    routed = nc.dram_tensor("routed", (NROWS, ROWW), F32, kind="Internal").ap()
    y_rows = nc.dram_tensor("y_rows", (2 * NTOK, D), F32, kind="Internal").ap()
    bias_rows = nc.dram_tensor("bias_rows", (2, NE * (DFF + D)), F32, kind="Internal").ap()
    build(nc, *args, out, routed, y_rows, bias_rows)
    return run_bass_kernel_spmd(nc, [arrays], core_ids=[0]).results[0]["out_0"]
```

```python
from contextlib import ExitStack

import numpy as np
import concourse.bass as bass
from concourse import mybir

F32 = mybir.dt.float32
F32R = mybir.dt.float32r
BF16 = mybir.dt.bfloat16
I32 = mybir.dt.int32
U32 = mybir.dt.uint32
ALU = mybir.AluOpType
ACT = mybir.ActivationFunctionType
AX_X = mybir.AxisListType.X

P = 128
NB = 32
NT = 256
D = 128
MEM = 32
NE = 8
DFF = 512
FB = DFF // P
TI = P // NB
NCH = NT // TI
BC = 4
NG = NCH // BC
NTOK = NB * NT
TR = 2 * P
REG = NTOK + TR
ROWW = 132
PAD_ROW = NE * REG
NROWS = PAD_ROW + TR
NTILE = 2 * NTOK // TR + NE - 1
HALF = NE * DFF // 2
RB = 4
XB = 4
SLOTS = 8
YSLOTS = 4
EC = 2 * BC
NP = NCH // EC
YB = 4
SKIP = 1 << 20
DECAY = 0.99
EPS = 1e-5


def shape_constants():
    p = np.arange(P)
    ti = p // NB
    before = ti[:, None] < ti[None, :]
    mask = np.where(before, DECAY ** (-1.0 - ti[:, None]) / NB, 0.0).astype(np.float32)
    mask = np.broadcast_to(mask, (P, P))
    kscale = (DECAY ** (TI - 1.0 - ti) / NB).astype(np.float32)[:, None]
    ident = np.eye(P, dtype=np.float32)
    tri = (p[:, None] < p[None, :]).astype(np.float32)
    eye8 = np.broadcast_to(np.arange(NE, dtype=np.float32), (P, NE))
    small = np.concatenate([eye8, eye8 * REG, kscale,
                            np.repeat(p[:, None], NE, axis=1), np.full((P, 1), EPS)], axis=1)
    square = np.concatenate([ident, mask, tri, np.ones((P, P), np.float32)], axis=1)
    chunk = np.arange(NCH)
    dest = (np.arange(2)[None, :, None] * NTOK + chunk[None, None, :] * P + p[:, None, None]).astype(np.int32)
    return {
        "c_square": np.ascontiguousarray(square),
        "c_small": np.ascontiguousarray(small.astype(np.float32)),
        "c_dest": np.ascontiguousarray(dest.reshape(P, 2 * NCH)),
    }


class Step:

    def __init__(self, turn, place, unroll):
        self.turn, self.place, self.unroll = turn + place // unroll, place % unroll, unroll

    def back(self, k):
        return Step(self.turn, self.place - k, self.unroll)

    @property
    def n(self):
        return self.turn * self.unroll + self.place

    def exists(self, count):
        return not isinstance(self.turn, int) or 0 <= self.n < count


def at_least(engine, sem, value):
    if not isinstance(value, int) or value > 0:
        engine.wait_ge(sem, value)


def settle(engine):
    engine.nop(nofuse=True)


def run_steps(engine, count, unroll, body):
    for place in range(unroll):
        body(Step(0, place, unroll))
    with engine.Fori(1, count // unroll) as turn:
        for place in range(unroll):
            body(Step(turn, place, unroll))
    for place in range(count % unroll):
        body(Step(count // unroll, place, unroll))


def straight(count, unroll, body):
    for n in range(count):
        body(Step(n // unroll, n % unroll, unroll))


def build(nc, x, Wq, Wk, Wv, Wo, gate, M0, Wg, bg, W1, b1, W2, b2, c, wmod,
          c_square, c_small, c_dest, out, routed, y_rows):
    with ExitStack() as ctx:
        def sb(name, shape, dt=F32):
            return ctx.enter_context(nc.sbuf_tensor(name, shape, dt))

        def sem(name):
            return ctx.enter_context(nc.semaphore(name))

        kv = ctx.enter_context(nc.psum_tensor("kv", [P, 2, 512], F32))
        bank = {i: ctx.enter_context(nc.psum_tensor(f"bank{i}", [P, 512], F32)) for i in (0, 1, 4, 5, 6, 7)}
        bank[2], bank[3] = kv[:, 0, :], kv[:, 1, :]

        X = sb("X", [P, NCH, D])
        W1hl = sb("W1hl", [P, NE, 2, DFF], F32R)
        W2hl = sb("W2hl", [P, NE * FB, 2 * D], F32R)
        bT = sb("bT", [P, NE, FB + 1])
        square = sb("square", [P, 4 * P])
        ident = square[:, 0:P]
        small = sb("small", [P, 3 * NE + 2])
        expert_id, expert_base = small[:, 0:NE], small[:, NE:2 * NE]
        kscale, tile_id = small[:, 2 * NE:2 * NE + 1], small[:, 2 * NE + 1:3 * NE + 1]
        eps = small[:, 3 * NE + 1:]
        dest = sb("dest", [P, 2, NCH], I32)
        tri = sb("tri", [P, P], BF16)
        ones = sb("ones", [P, P], BF16)
        mod = sb("mod", [P, 6, D])
        wqkv = sb("wqkv", [P, 2 * MEM + D])
        WgS = sb("WgS", [P, NE])
        bgS = sb("bgS", [P, NE])
        top = sb("top", [P, NCH, 8])
        pairw = sb("pairw", [P, 2, NCH])
        stage = sb("stage", [P, 2, HALF])
        vS = sb("vS", [P, 2, BC, D])
        kT = sb("kT", [MEM, 2, BC * P])
        early = vS[:].rearrange("p b c d -> p (b c d)")
        cS = early[0:NB, 0:3 * D].rearrange("p (i d) -> p i d", i=3)
        scT = early[:, 3 * D:4 * D]
        wsm = early[:, 4 * D:7 * D + MEM + 1]
        woT, b1S, b2S = kT[:, 0, 0:D], kT[:, 0, D:2 * D], kT[0:NE, 0, 2 * D:3 * D]
        M0S = sb("M0S", [MEM, MEM])
        hn = sb("hn", [P, 2, BC, D])
        wmS = stage[:, 1, 0:6 * D]
        hT = sb("hT", [P, BC * P])
        qT = sb("qT", [MEM, 2, BC * P])
        kS = sb("kS", [P, 2, BC, MEM])
        aS = sb("aS", [P, BC, P])
        att = sb("att", [P, BC, D])
        Mst = sb("Mst", [MEM, 2, BC, D])
        st6 = sb("st6", [P, 2 * BC, 6])
        mv = sb("mv", [P, 2 * BC, 2])
        rs = sb("rs", [P, 4, 2 * BC])
        rows = sb("rows", [P, RB, 2, BC, ROWW])
        h2T = sb("h2T", [P, BC * P])
        lg = sb("lg", [P, BC, NE])
        chosen = sb("chosen", [P, BC, 8], U32)
        chosen_f = sb("chosen_f", [P, BC, 8])
        oh = sb("oh", [P, 2, BC, NE])
        T = sb("T", [P, BC, NE], BF16)
        cum = sb("cum", [P, 2, NE])
        cumb = sb("cumb", [P, NE], BF16)
        rk = sb("rk", [P, BC, NE])
        rk2 = sb("rk2", [P, 2, BC, NE])
        posf = sb("posf", [P, 2 * BC])
        pos = sb("pos", [P, RB, 2 * BC], I32)
        padrow = sb("padrow", [P, ROWW])
        padpos = sb("padpos", [P, NE], I32)
        cnt_i = sb("cnt_i", [P, NE], I32)
        tiles_f = sb("tiles_f", [P, 3, NE])
        beyond = sb("beyond", [P, 2, NE])
        tab = sb("tab", [P, 2])
        tile_row = sb("tile_row", [1, NTILE], I32)
        tile_exp = sb("tile_exp", [1, NTILE], I32)
        tin = rows[:].rearrange("p r k c w -> p (r k c) w")[:, 0:2 * SLOTS, :]
        tin = tin.rearrange("p (s h) w -> p s h w", h=2)
        W1s = sb("W1s", [P, 2, 2, DFF], F32R)
        W2s = sb("W2s", [P, 2, FB, 2 * D], F32R)
        bs = sb("bs", [P, 4, FB + 1])
        th = sb("th", [P, 2, TR], F32R)
        tl = sb("tl", [P, 2, TR], F32R)
        g = stage[:, 0].rearrange("p (b f) -> p b f", b=2)
        gh = sb("gh", [P, 2, FB * TR], F32R)
        gl = sb("gl", [P, 2, FB * TR], F32R)
        yT = att[:].rearrange("p c d -> p (c d)").rearrange("p (b w) -> p b w", b=2)
        ysb = hn[:].rearrange("p a c d -> p (a c) d").rearrange("p (s h) d -> p s h d", h=2)
        yb = [part.rearrange("p (k c d) -> p k c d", k=2, c=EC) for part in (
            stage[:, 0], stage[:, 1], rows[:].rearrange("p r k c w -> p (r k c w)")[:, 0:2 * EC * D],
            rows[:].rearrange("p r k c w -> p (r k c w)")[:, 2 * EC * D:4 * EC * D])]

        S = {n: sem(n) for n in (
            "consts_in", "wmod_in", "w1_in0", "w1_in1", "w2_in0", "w2_in1", "act_setup",
            "silu_ready", "transposed", "copied", "products", "setup_done", "split_hi", "split_lo", "zeroed",
            "b_ps", "w1_copied", "w2_copied", "yT_ready", "yt_ps",
            "ln_var", "ln_sd", "ln_ready", "z1", "z2", "h_ready", "hT_ps", "hT_ready", "qk_ps", "v_ps",
            "q_ready", "k_ready", "v_ready", "s_ps", "a_ready", "u_ps", "m_ready", "o_ps", "o_read",
            "h2_ready", "h2_copied", "dest_set", "h2T_ps", "h2T_ready", "lg_ps", "t_ready", "rk_ps", "pos_ready",
            "dve", "cum_ready", "cnt_ps", "tab_cols", "tab_ps", "pads_ready", "pads_in", "table_ready",
            "exp_in", "exp_ready", "w_ready",
            "th_ps", "th_ready", "mm1", "gelu", "gh_ready", "gl_ready", "y_ps", "y_ready",
            "y0_scaled", "y_weighted", "y_summed", "sum_ready", "out_done",
        )}
        x_in = [sem(f"x_in{i}") for i in range(XB)]
        rows_out = [sem(f"rows_out{i}") for i in range(RB)]
        tile_in = [sem(f"tile_in{i}") for i in range(SLOTS)]
        tile_out = [sem(f"tile_out{i}") for i in range(YSLOTS)]
        y_in = [sem(f"y_in{i}") for i in range(YB)]

        x_v = x.rearrange("b (n c t) d -> n t b c d", c=BC, t=TI)
        out_v = out.rearrange("b (n c t) d -> n t b c d", c=EC, t=TI)
        y_v = y_rows.rearrange("(k n c p) d -> k n p c d", k=2, p=P, c=EC)

        loads = ((square[:], c_square), (small[:], c_small), (cS[:, 0, :], c), (WgS[:], Wg), (M0S[:], M0),
                 (bgS[:], bg.rearrange("(a e) -> a e", a=1).broadcast_to((P, NE))),
                 (wsm[0:MEM, 0:D], Wq), (wsm[0:MEM, D:2 * D], Wk), (wsm[0:MEM, 2 * D:3 * D], Wv),
                 (wsm[:, 3 * D:3 * D + MEM], Wo),
                 (wsm[:, 3 * D + MEM:], gate.rearrange("(a e) -> a e", a=1).broadcast_to((P, 1))),
                 (b1S, b1.rearrange("e (f p) -> (e f) p", p=P)),
                 (b2S, b2),
                 (dest[:].rearrange("p k c -> p (k c)"), c_dest))
        CONSTS = 16 * len(loads)

        def half(n):
            return yb[n // 2 % YB][:, :, n % 2 * BC:(n % 2 + 1) * BC, :]

        def has(n):
            return 0 <= n < NG

        def normed(n):
            return has(n) or has(n - 2)

        def norm_columns(n):
            return slice(0 if has(n) else BC, 2 * BC if has(n - 2) else BC)

        def rows_sent(buffer, groups):
            return 16 * 2 * BC * len(range(buffer, groups, RB))

        def tile_rows(row):
            return routed[bass.ds(row, TR), :].rearrange("(h p) w -> p h w", h=2)

        def padding():
            return padrow[:].rearrange("p (a w) -> p a w", a=1).broadcast_to((P, 2, ROWW))

        def put_pads(engine, experts):
            engine.wait_ge(S["pads_ready"], 1)
            settle(engine)
            for e in experts:
                row = engine.value_load(padpos[0:1, e:e + 1], min_val=0, max_val=PAD_ROW)
                engine.dma_start(tile_rows(row), padding()).then_inc(S["pads_in"], 16)

        def y_left(j, back):
            per_turn = SLOTS // YSLOTS
            return 32 * (j.turn * per_turn + j.place // YSLOTS - back // YSLOTS + 1)

        block = ctx.enter_context(nc.Block())

        @block.sync
        def _(sp):
            for dst, src in loads[0::2]:
                sp.dma_start(dst, src).then_inc(S["consts_in"], 16)
            sp.dma_start(wmS, wmod).then_inc(S["wmod_in"], 16)

            def load_x(n):
                at_least(sp, S["hT_ps"], n.n - XB + 1)
                settle(sp)
                for t in range(TI):
                    sp.dma_start(X[t * NB:(t + 1) * NB, bass.ds(n.n * BC, BC), :], x_v[n.n, t]).then_inc(
                        x_in[n.place], 16)

            HE = NE // 2
            w1_v, w2_v = W1.rearrange("e d f -> d e f"), W2.rearrange("e (f p) d -> p e f d", p=P)
            for i in range(2):
                load_x(Step(0, 2 * i, XB))
                load_x(Step(0, 2 * i + 1, XB))
                if i == 1:
                    sp.wait_ge(S["products"], 1)
                sp.dma_start(stage[:, i, :].rearrange("p (e f) -> p e f", e=HE),
                             w1_v[:, i * HE:(i + 1) * HE]).then_inc(S[f"w1_in{i}"], 16)
            for i in range(2):
                load_x(Step(1, 2 * i, XB))
                load_x(Step(1, 2 * i + 1, XB))
                sp.wait_ge(S["split_lo"], i + 1)
                sp.dma_start(stage[:, i, :].rearrange("p (e f d) -> p e f d", e=HE, f=FB),
                             w2_v[:, i * HE:(i + 1) * HE]).then_inc(S[f"w2_in{i}"], 16)
            with sp.Fori(2, NG // XB) as turn:
                for i in range(XB):
                    load_x(Step(turn, i, XB))
            sp.wait_ge(S["zeroed"], 3)
            sp.dma_start(tile_rows(PAD_ROW), padding()).then_inc(S["pads_in"], 16)
            put_pads(sp, range(0, NE // 2))

            sp.wait_ge(S["table_ready"], 2)
            sp.wait_ge(S["pads_in"], 16 * (NE + 1))
            for s in range(RB):
                sp.wait_ge(rows_out[s], rows_sent(s, NG))

            def load_tile(j):
                at_least(sp, S["th_ps"], j.n - SLOTS + 1)
                settle(sp)
                at_least(sp, tile_out[j.place % YSLOTS], y_left(j, SLOTS))
                settle(sp)
                row = sp.value_load(tile_row[0:1, bass.ds(j.n, 1)], min_val=0, max_val=PAD_ROW)
                sp.dma_start(tin[:, j.place], tile_rows(row)).then_inc(tile_in[j.place], 16)
            run_steps(sp, NTILE, SLOTS, load_tile)

            for s in range(YSLOTS):
                sp.wait_ge(tile_out[s], 32 * len(range(s, NTILE, YSLOTS)))

            def load_y(n):
                for k in range(2):
                    sp.dma_start(yb[n % YB][:, k], y_v[k, n]).then_inc(y_in[n % YB], 16)

            for n in range(YB):
                load_y(n)
            for n in range(NP):
                sp.wait_ge(S["sum_ready"], 2 * n + 2)
                for t in range(TI):
                    sp.dma_start(out_v[n, t], X[t * NB:(t + 1) * NB, n * EC:(n + 1) * EC, :]).then_inc(
                        S["out_done"], 16)
                if n + YB < NP:
                    load_y(n + YB)
            sp.wait_ge(S["out_done"], 16 * TI * NP)

        @block.gpsimd
        def _(pool):
            pool.memset(padrow[:, 0:D], 0.0).then_inc(S["zeroed"], 1)
            pool.memset(padrow[:, D:].bitcast(I32), SKIP).then_inc(S["zeroed"], 1)
            pool.memset(rows[:, :, :, :, D + 1:], 0.0).then_inc(S["zeroed"], 1)
            pool.wait_ge(S["consts_in"], CONSTS)
            def split_w1(i):
                pool.wait_ge(S["split_hi"], i + 1)
                part = W1hl[:, i * NE // 2:(i + 1) * NE // 2]
                pool.tensor_tensor(part[:, :, 1], stage[:, i, :].rearrange("p (e f) -> p e f", f=DFF),
                                   part[:, :, 0].bitcast(F32), ALU.subtract).then_inc(S["split_lo"], 1)

            def split_w2(i):
                pool.wait_ge(S["split_hi"], i + 3)
                part = W2hl[:, i * NE * FB // 2:(i + 1) * NE * FB // 2, :]
                pool.tensor_tensor(part[:, :, D:2 * D], stage[:, i, :].rearrange("p (e d) -> p e d", d=D),
                                   part[:, :, 0:D].bitcast(F32), ALU.subtract).then_inc(S["split_lo"], 1)

            split_w1(0)
            split_w1(1)
            for n in range(NG):
                at_least(pool, rows_out[n % RB], rows_sent(n % RB, n))
                for k in range(2):
                    ins = pool.tensor_copy(rows[:, n % RB, k, :, D:D + 1].bitcast(I32).rearrange("p c a -> p (c a)"),
                                           dest[:, k, n * BC:(n + 1) * BC])
                ins.then_inc(S["dest_set"], 1)
                pool.wait_ge(S["pos_ready"], n + 1)
                pool.wait_ge(S["dest_set"], n + 1)
                pool.wait_ge(S["h2_ready"], n + 1)
                pool.wait_ge(S["h2_copied"], n + 1)
                for k in range(2):
                    for j in range(BC):
                        pool.indirect_dma_start(
                            routed, bass.IndirectOffsetOnAxis(pos[:, n % RB, k * BC + j:k * BC + j + 1], 0),
                            rows[:, n % RB, k, j, :], None).then_inc(rows_out[n % RB], 16)
                if n < 2:
                    split_w2(n)

            def put_y(j):
                pool.wait_ge(S["y_ready"], j.n + 1)
                settle(pool)
                for h in range(2):
                    pool.indirect_dma_start(
                        y_rows, bass.IndirectOffsetOnAxis(tin[:, j.place, h, D:D + 1].bitcast(I32), 0),
                        ysb[:, j.place % YSLOTS, h, :], None, bounds_check=2 * NTOK - 1, oob_is_err=False).then_inc(
                            tile_out[j.place % YSLOTS], 16)
            run_steps(pool, NTILE, SLOTS, put_y)

            for n in range(2 * NP):
                pool.wait_ge(S["y_summed"], n + 1)
                xs = X[:, n * BC:(n + 1) * BC, :]
                pool.tensor_tensor(xs, xs, half(n)[:, 0], ALU.add).then_inc(S["sum_ready"], 1)

        @block.scalar
        def _(act):
            for dst, src in loads[1::2]:
                act.dma_start(dst, src).then_inc(S["consts_in"], 16)
            act.wait_ge(S["consts_in"], CONSTS)
            act.activation(cS[:, 1, :], cS[:, 0, :], ACT.Exp, scale=-1.0).then_inc(S["act_setup"], 1)
            act.activation(wsm[:, 3 * D + MEM:], wsm[:, 3 * D + MEM:], ACT.Exp, scale=-1.0).then_inc(
                S["act_setup"], 1)

            def norm_roots(n):
                at = norm_columns(n)
                act.wait_ge(S["ln_var"], n + 1)
                act.activation(rs[:, 0, at], mv[:, at, 1], ACT.Sqrt, bias=eps).then_inc(S["ln_sd"], 1)

            def normalize(n, half, dst, done):
                for j in range(BC):
                    i = half * BC + j
                    ins = act.activation(dst[:, j, :], X[:, n * BC + j, :], ACT.Identity, scale=rs[:, 1, i:i + 1],
                                         bias=rs[:, 3, i:i + 1])
                ins.then_inc(S[done], 1)

            def steps(n):
                f, m = n, n - 2
                act.wait_ge(S["ln_ready"], n + 1)
                if has(f):
                    at_least(act, S["hT_ps"], f - 1)
                    normalize(f, 0, hn[:, f % 2], "z1")
                if has(m):
                    at_least(act, rows_out[m % RB], rows_sent(m % RB, m))
                    at_least(act, S["h2T_ps"], m - RB + 1)
                    normalize(m, 1, rows[:, m % RB, 0, :, 0:D], "z2")
                if has(f):
                    b = f % 2
                    act.wait_ge(S["hT_ps"], f + 1)
                    at_least(act, S["v_ps"], f)
                    act.activation(hT[:], bank[0][:], ACT.Copy).then_inc(S["hT_ready"], 1)
                    act.wait_ge(S["qk_ps"], f + 1)
                    at_least(act, S["o_ps"], f - 1)
                    q = bank[1][0:MEM, :].rearrange("p (c t b) -> p c t b", c=BC, t=TI)
                    for t in range(TI):
                        ins = act.activation(qT[:, b].rearrange("p (c t b) -> p c t b", c=BC, t=TI)[:, :, t, :],
                                             q[:, :, t, :], ACT.Copy, scale=DECAY ** t)
                    ins.then_inc(S["q_ready"], 1)
                    act.activation(kT[:, b, :], bank[1][MEM:2 * MEM, :], ACT.Copy).then_inc(S["k_ready"], 1)
                if has(m):
                    act.wait_ge(S["h2T_ps"], m + 1)
                    at_least(act, S["lg_ps"], m)
                    act.activation(h2T[:], bank[5][:], ACT.Copy).then_inc(S["h2T_ready"], 1)
                if normed(n + 1):
                    norm_roots(n + 1)
                if has(f):
                    act.wait_ge(S["v_ps"], f + 1)
                    k_v = kv[:, :, 0:2 * (MEM + D)].rearrange("p a (c w) -> p a c w", c=2)
                    act.activation(vS[:, b].rearrange("p (a c) d -> p a c d", a=2), k_v[:, :, :, MEM:],
                                   ACT.Copy).then_inc(S["v_ready"], 1)
                    act.activation(kS[:, b].rearrange("p (a c) d -> p a c d", a=2), k_v[:, :, :, 0:MEM],
                                   ACT.Copy, scale=kscale).then_inc(S["v_ready"], 1)
                if has(m):
                    act.wait_ge(S["h2_ready"], m + 1)
                    act.activation(rows[:, m % RB, 1, :, 0:D], rows[:, m % RB, 0, :, 0:D], ACT.Copy).then_inc(
                        S["h2_copied"], 1)

            def split_w1(i):
                act.wait_ge(S[f"w1_in{i}"], 16)
                act.activation(W1hl[:, i * NE // 2:(i + 1) * NE // 2, 0],
                               stage[:, i, :].rearrange("p (e f) -> p e f", f=DFF), ACT.Copy).then_inc(
                                   S["split_hi"], 1)

            def split_w2(i):
                act.wait_ge(S[f"w2_in{i}"], 16)
                act.activation(W2hl[:, i * NE * FB // 2:(i + 1) * NE * FB // 2, 0:D],
                               stage[:, i, :].rearrange("p (e d) -> p e d", d=D), ACT.Copy).then_inc(
                                   S["split_hi"], 1)

            norm_roots(0)
            for n in range(NG + 2):
                steps(n)
                if n in (2, 3):
                    split_w1(n - 2)
                elif n in (4, 5):
                    split_w2(n - 4)
            act.wait_ge(S["exp_in"], 1)
            act.activation(pairw[:, 1, :], pairw[:, 0, :], ACT.Exp).then_inc(S["exp_ready"], 1)

            act.activation(rs[:, 0, 0:1], mv[:, 0, 1:2], ACT.Gelu)
            put_pads(act, range(NE // 2, NE))

            def tile(n):
                j = n.back(1)
                b = j.place % 2
                if j.exists(NTILE):
                    at_least(act, S["gl_ready"], j.n - 1)
                    for f in range(FB):
                        if f % 2 == 0:
                            act.wait_ge(S["mm1"], FB * j.n + f + 2)
                        act.activation(g[:, b, f * TR:(f + 1) * TR],
                                       bank[2 + 2 * b + f // 2][:, f % 2 * TR:(f % 2 + 1) * TR], ACT.Gelu,
                                       bias=bs[:, j.place % 4, f:f + 1]).then_inc(S["gelu"], 1)
                    act.wait_ge(S["gelu"], FB * j.n + FB)
                    at_least(act, S["y_ps"], j.n - 1)
                    act.activation(gh[:, b, :], g[:, b, :], ACT.Copy).then_inc(S["gh_ready"], 1)
                j = n.back(2)
                b = j.place % 2
                if j.exists(NTILE):
                    act.wait_ge(S["y_ps"], j.n + 1)
                    at_least(act, S["yt_ps"], j.n - 1)
                    act.activation(yT[:, b, :], bank[6 + b][:, 0:TR], ACT.Identity,
                                   bias=bs[:, j.place % 4, FB:FB + 1]).then_inc(S["yT_ready"], 1)
                j = n.back(3)
                b = j.place % 2
                if j.exists(NTILE):
                    act.wait_ge(S["yt_ps"], j.n + 1)
                    at_least(act, tile_out[j.place % YSLOTS], y_left(j, YSLOTS))
                    act.activation(ysb[:, j.place % YSLOTS], bank[6 + b][:, TR:2 * TR].rearrange(
                        "p (h d) -> p h d", h=2), ACT.Copy).then_inc(S["y_ready"], 1)
            act.wait_ge(S["split_lo"], 4)
            straight(NTILE + 3, SLOTS, tile)

            act.wait_ge(S["w_ready"], 1)
            for n in range(2 * NP):
                act.wait_ge(y_in[n // 2 % YB], (n // 2 // YB + 1) * 32)
                for j in range(BC):
                    c = n * BC + j
                    ins = act.activation(half(n)[:, 0, j, :], half(n)[:, 0, j, :], ACT.Copy,
                                         scale=pairw[:, 0, c:c + 1])
                ins.then_inc(S["y0_scaled"], 1)

        @block.vector
        def _(dve):
            chain = [0]

            def mark(ins):
                chain[0] += 1
                ins.then_inc(S["dve"], 1)
                return chain[0]

            def after(count):
                dve.wait_ge(S["dve"], count)

            def then(ins):
                mark(ins)
                dve.wait_ge(S["dve"], chain[0])

            dve.wait_ge(S["consts_in"], CONSTS)
            mark(dve.tensor_copy(tri[:], square[:, 2 * P:3 * P]))
            mark(dve.tensor_copy(ones[:], square[:, 3 * P:4 * P]))
            dve.wait_ge(S["b_ps"], 1)
            mark(dve.tensor_copy(bT[:, :, 0:FB], bank[1][:, 0:NE * FB].rearrange("p (e f) -> p e f", e=NE)))
            mark(dve.tensor_copy(bT[:, :, FB], bank[1][:, NE * FB:NE * (FB + 1)]))
            dve.wait_ge(S["act_setup"], 2)
            gt = wsm[:, 3 * D + MEM:]
            then(dve.tensor_scalar(cS[:, 2, :], cS[:, 1, :], 1.0, None, ALU.add))
            then(dve.reciprocal(cS[:, 1, :], cS[:, 2, :]))
            dve.tensor_tensor(cS[:, 2, :], cS[:, 1, :], cS[:, 0, :], ALU.mult).then_inc(S["silu_ready"], 1)
            then(dve.tensor_scalar(gt, gt, 1.0, None, ALU.add))
            then(dve.reciprocal(gt, gt))
            dve.wait_ge(S["transposed"], 1)
            dve.tensor_copy(scT[:].rearrange("p (t b) -> p t b", t=TI),
                            bank[0][:, 0:NB].rearrange("p (t b) -> p t b", t=1).broadcast_to(
                                (P, TI, NB))).then_inc(S["copied"], 1)
            dve.tensor_copy(wqkv[:, 0:2 * MEM], bank[0][:, NB:NB + 2 * MEM]).then_inc(S["copied"], 1)
            dve.tensor_copy(woT[:], bank[0][0:MEM, P:P + D]).then_inc(S["copied"], 1)
            def per_token(i):
                return mod[:, i:i + 1, :].broadcast_to((P, BC, D))

            def statistics(n):
                f, m = n, n - 2
                if has(f):
                    dve.wait_ge(x_in[f % XB], (f // XB + 1) * (TI * 16))
                    for j in range(BC):
                        mark(dve.bn_stats(st6[:, j, :], X[:, f * BC + j, :]))
                if has(m):
                    for j in range(BC):
                        mark(dve.bn_stats(st6[:, BC + j, :], X[:, m * BC + j, :]))
                at = norm_columns(n)
                dve.wait_ge(S["dve"], chain[0])
                for i in range(at.start, at.stop):
                    ins = dve.bn_aggr(mv[:, i, :], st6[:, i, :])
                ins.then_inc(S["ln_var"], 1)

            def roots(n):
                at = norm_columns(n)
                sd, r, t, nb = (rs[:, i, at] for i in range(4))
                mean, var = mv[:, at, 0], mv[:, at, 1]
                dve.wait_ge(S["ln_sd"], n + 1)
                then(dve.reciprocal(r, sd))
                then(dve.scalar_tensor_tensor(out=t, in0=r, scalar=-0.5, in1=r, op0=ALU.mult, op1=ALU.mult))
                then(dve.scalar_tensor_tensor(out=t, in0=var, scalar=EPS, in1=t, op0=ALU.add, op1=ALU.mult))
                then(dve.scalar_tensor_tensor(out=r, in0=t, scalar=1.5, in1=r, op0=ALU.add, op1=ALU.mult))
                dve.scalar_tensor_tensor(out=nb, in0=mean, scalar=-1.0, in1=r, op0=ALU.mult,
                                         op1=ALU.mult).then_inc(S["ln_ready"], 1)


            def state(n, j):
                if j > 0:
                    dve.wait_ge(S["m_ready"], n * BC + j)
                to = Mst[:, n % 2, j + 1, :] if j < BC - 1 else Mst[:, 1 - n % 2, 0, :]
                dve.scalar_tensor_tensor(out=to, in0=Mst[:, n % 2, j, :], scalar=DECAY ** TI,
                                         in1=bank[1][0:MEM, j * D:(j + 1) * D], op0=ALU.mult,
                                         op1=ALU.add).then_inc(S["m_ready"], 1)

            def choice_and_states(l, n):
                if has(l):
                    dve.wait_ge(S["lg_ps"], l + 1)
                    c = mark(dve.tensor_tensor(
                        lg[:], bank[6][:, 0:BC * NE].rearrange("p (c e) -> p c e", c=BC),
                        bgS[:].rearrange("p (a e) -> p a e", a=1).broadcast_to((P, BC, NE)), ALU.add))
                if has(n):
                    dve.wait_ge(S["s_ps"], n + 1)
                    at_least(dve, S["o_ps"], n)
                    dve.tensor_tensor(aS[:], bank[4][:].rearrange("p (c t) -> p c t", c=BC),
                                      square[:, P:2 * P].rearrange("p (a t) -> p a t", a=1).broadcast_to(
                                          (P, BC, P)), ALU.mult).then_inc(S["a_ready"], 1)
                if has(l):
                    after(c)
                    for j in range(BC):
                        c = mark(dve.max(top[:, l * BC + j, :], lg[:, j, :]))
                if has(n):
                    dve.wait_ge(S["u_ps"], n + 1)
                    state(n, 0)
                if has(l):
                    after(c)
                    for j in range(BC):
                        c = mark(dve.max_index(chosen[:, j, :], top[:, l * BC + j, :], lg[:, j, :]))
                if has(n):
                    state(n, 1)
                if has(l):
                    after(c)
                    c = mark(dve.tensor_copy(chosen_f[:], chosen[:]))
                if has(n):
                    state(n, 2)
                if has(l):
                    after(c)
                    c = mark(dve.tensor_tensor(
                        oh[:].rearrange("p k c e -> p c k e"), chosen_f[:, :, 0:2].rearrange(
                            "p c (k a) -> p c k a", a=1).broadcast_to((P, BC, 2, NE)),
                        expert_id.rearrange("p (a b e) -> p a b e", a=1, b=1).broadcast_to((P, BC, 2, NE)),
                        ALU.is_equal))
                if has(n):
                    state(n, 3)
                if has(l):
                    after(c)
                    dve.tensor_tensor(T[:], oh[:, 0], oh[:, 1], ALU.add).then_inc(S["t_ready"], 1)

            def modulation_and_places(f, m, l):
                z1, z2 = hn[:, f % 2], rows[:, m % RB, 0, :, 0:D]
                if has(f):
                    dve.wait_ge(S["z1"], f + 1)
                    k = mark(dve.tensor_tensor(z1, z1, per_token(1), ALU.mult))
                if has(l):
                    dve.wait_ge(S["rk_ps"], l + 1)
                    t = mark(dve.tensor_reduce(cum[:, 1, :], T[:].rearrange("p c e -> p e c"), AX_X, ALU.add))
                    c = mark(dve.tensor_tensor(rk[:], bank[6][:, P:P + BC * NE].rearrange("p (c e) -> p c e", c=BC),
                                               expert_base.rearrange("p (a e) -> p a e", a=1).broadcast_to(
                                                   (P, BC, NE)), ALU.add))
                if has(f):
                    after(k)
                    dve.tensor_tensor(z1, z1, per_token(0), ALU.add).then_inc(S["h_ready"], 1)
                if has(l):
                    after(t)
                    t = mark(dve.tensor_tensor(cum[:, 0, :], cum[:, 0, :], cum[:, 1, :], ALU.add))
                    after(c)
                    c = mark(dve.tensor_tensor(
                        rk2[:].rearrange("p k c e -> p k (c e)"),
                        rk[:].rearrange("p (a c) e -> p a (c e)", a=1).broadcast_to((P, 2, BC * NE)),
                        oh[:].rearrange("p k c e -> p k (c e)"), ALU.mult))
                if has(m):
                    dve.wait_ge(S["z2"], m + 1)
                    k = mark(dve.tensor_tensor(z2, z2, per_token(4), ALU.mult))
                if has(l):
                    after(t)
                    dve.tensor_copy(cumb[:], cum[:, 0, :]).then_inc(S["cum_ready"], 1)
                    after(c)
                    c = mark(dve.tensor_reduce(posf[:], rk2[:].rearrange("p k c e -> p (k c) e"), AX_X, ALU.add))
                if has(m):
                    after(k)
                    dve.tensor_tensor(z2, z2, per_token(3), ALU.add).then_inc(S["h2_ready"], 1)
                if has(l):
                    after(c)
                    at_least(dve, rows_out[l % RB], rows_sent(l % RB, l))
                    dve.tensor_copy(pos[:, l % RB, :], posf[:]).then_inc(S["pos_ready"], 1)

            def residual(n):
                dve.wait_ge(S["o_ps"], n + 1)
                dve.tensor_tensor(att[:], bank[7][:].rearrange("p (c d) -> p c d", c=BC), per_token(2),
                                  ALU.mult).then_inc(S["o_read"], 1)
                dve.wait_ge(S["o_read"], n + 1)
                xs = X[:, n * BC:(n + 1) * BC, :]
                then(dve.tensor_tensor(xs, xs, att[:], ALU.add))

            statistics(0)
            roots(0)
            dve.wait_ge(S["products"], 1)
            then(dve.memset(cum[:], 0.0))
            mark(dve.memset(cumb[:], 0.0))
            mark(dve.tensor_copy(wqkv[:, 2 * MEM:], bank[2][:, 0:D]))
            mark(dve.tensor_copy(Mst[:, 0, 0, :], bank[3][0:MEM, 0:D]))
            mark(dve.tensor_copy(mod[:, 0:3, :], bank[4][:, 0:3 * D].rearrange("p (s d) -> p s d", s=3)))
            then(dve.tensor_copy(mod[:, 3:6, :], bank[5][:, 0:3 * D].rearrange("p (s d) -> p s d", s=3)))
            for i in (1, 4):
                then(dve.tensor_scalar(mod[:, i, :], mod[:, i, :], 1.0, None, ALU.add))
            for i in (2, 5):
                mark(dve.tensor_scalar(att[:, 0, :], mod[:, i, :], 0.0, 2.0, ALU.is_ge, ALU.mult))
                then(dve.tensor_scalar(att[:, 2, :], mod[:, i, :], -1.0, 0.25, ALU.mult, ALU.max))
                then(dve.tensor_tensor(att[:, 1, :], mod[:, i, :], att[:, 2, :], ALU.max))
                then(dve.scalar_tensor_tensor(out=mod[:, i, :], in0=att[:, 0, :], scalar=-1.0, in1=att[:, 1, :],
                                              op0=ALU.add, op1=ALU.mult))
            dve.tensor_scalar(mod[:, 2, :], mod[:, 2, :], gt, None, ALU.mult).then_inc(S["setup_done"], 1)
            dve.wait_ge(S["setup_done"], 1)

            for n in range(NG + 3):
                if has(n - 2):
                    residual(n - 2)
                if n > 0 and normed(n):
                    statistics(n)
                    roots(n)
                choice_and_states(n - 3, n - 1)
                modulation_and_places(n, n - 2, n - 3)

            dve.wait_ge(S["cnt_ps"], 1)
            cnt = bank[6][:, 2 * P:2 * P + NE]
            dve.wait_ge(S["zeroed"], 3)
            dve.tensor_tensor(padpos[:], cnt, expert_base, ALU.add).then_inc(S["pads_ready"], 1)
            then(dve.tensor_scalar(cnt_i[:], cnt, float(TR - 1), None, ALU.add))
            tiles, upto, jump = tiles_f[:, 0, :], tiles_f[:, 1, :], tiles_f[:, 2, :]
            then(dve.tensor_scalar(cnt_i[:], cnt_i[:], TR.bit_length() - 1, None, ALU.logical_shift_right))
            then(dve.tensor_copy(tiles, cnt_i[:]))
            mark(dve.tensor_scalar(jump, tiles, float(-TR), float(REG), ALU.mult, ALU.add))
            then(dve.tensor_tensor_scan(upto, square[:, 3 * P:3 * P + NE], tiles, 0.0, ALU.mult, ALU.add))
            then(dve.tensor_tensor(beyond[:, 0], tile_id, upto, ALU.is_ge))
            then(dve.tensor_tensor(beyond[:, 1], beyond[:, 0], jump, ALU.mult))
            then(dve.tensor_reduce(tab[:], beyond[:], AX_X, ALU.add))
            then(dve.scalar_tensor_tensor(out=tab[:, 1:2], in0=tile_id[:, 0:1], scalar=float(TR), in1=tab[:, 1:2],
                                          op0=ALU.mult, op1=ALU.add))
            mark(dve.tensor_scalar(tab[:, 0:1], tab[:, 0:1], float(NE - 1), None, ALU.min))
            dve.tensor_scalar(tab[:, 1:2], tab[:, 1:2], float(PAD_ROW), None, ALU.min).then_inc(S["tab_cols"], 1)
            dve.tensor_tensor(pairw[:, 0, :], top[:, :, 1], top[:, :, 0], ALU.subtract).then_inc(S["exp_in"], 1)
            dve.wait_ge(S["tab_ps"], 1)
            dve.tensor_copy(tile_exp[:], bank[0][0:1, 0:NTILE]).then_inc(S["table_ready"], 1)
            dve.tensor_copy(tile_row[:], bank[0][0:1, P:P + NTILE]).then_inc(S["table_ready"], 1)
            dve.wait_ge(S["exp_ready"], 1)
            then(dve.tensor_scalar(pairw[:, 0, :], pairw[:, 1, :], 1.0, None, ALU.add))
            then(dve.reciprocal(pairw[:, 0, :], pairw[:, 0, :]))
            dve.tensor_tensor(pairw[:, 1, :], pairw[:, 1, :], pairw[:, 0, :], ALU.mult).then_inc(S["w_ready"], 1)

            expert = {}

            def tile(n):
                j = n.back(1)
                b = j.place % 2
                if j.exists(NTILE):
                    at_least(dve, S["y_ps"], j.n - 1)
                    dve.tensor_copy(W2s[:, b], W2hl[:, bass.ds(expert.pop(j.n) * FB, FB), :]).then_inc(
                        S["w2_copied"], 1)
                j = n.back(2)
                b = j.place % 2
                if j.exists(NTILE):
                    dve.wait_ge(S["gh_ready"], j.n + 1)
                    at_least(dve, S["y_ps"], j.n - 1)
                    dve.tensor_tensor(gl[:, b, :], g[:, b, :], gh[:, b, :].bitcast(F32),
                                      ALU.subtract).then_inc(S["gl_ready"], 1)
                j, b = n, n.place % 2
                if j.exists(NTILE):
                    dve.wait_ge(S["th_ps"], j.n + 1)
                    at_least(dve, S["mm1"], FB * (j.n - 1))
                    dve.tensor_copy(th[:, b, :], bank[b][:, 0:TR]).then_inc(S["th_ready"], 1)
                    e = dve.value_load(tile_exp[0:1, j.n:j.n + 1], min_val=0, max_val=NE - 1)
                    expert[j.n] = e
                    dve.tensor_copy(W1s[:, b].rearrange("p h f -> p (h f)"),
                                    W1hl[:, bass.ds(e, 1)].rearrange("p a h f -> p (a h f)")).then_inc(
                                        S["w1_copied"], 1)
                    dve.wait_ge(S["th_ready"], j.n * 2 + 1)
                    dve.tensor_tensor(tl[:, b, :], bank[b][:, 0:TR], th[:, b, :].bitcast(F32),
                                      ALU.subtract).then_inc(S["th_ready"], 1)
                    at_least(dve, S["yT_ready"], j.n - 3)
                    dve.tensor_copy(bs[:, j.place % 4, :],
                                    bT[:, bass.ds(e, 1), :].rearrange("p a f -> p (a f)")).then_inc(
                                        S["w1_copied"], 1)
            dve.wait_ge(S["table_ready"], 2)
            dve.wait_ge(S["split_lo"], 4)
            straight(NTILE + 2, SLOTS, tile)

            dve.wait_ge(S["w_ready"], 1)
            for n in range(2 * NP):
                y = half(n)
                dve.wait_ge(S["y0_scaled"], n + 1)
                for j in range(BC):
                    c = n * BC + j
                    ins = dve.scalar_tensor_tensor(out=y[:, 0, j, :], in0=y[:, 1, j, :], scalar=pairw[:, 1, c:c + 1],
                                                   in1=y[:, 0, j, :], op0=ALU.mult, op1=ALU.add)
                ins.then_inc(S["y_weighted"], 1)
                dve.wait_ge(S["y_weighted"], n + 1)
                dve.tensor_tensor(y[:, 0], y[:, 0], per_token(5), ALU.mult).then_inc(S["y_summed"], 1)

        @block.tensor
        def _(pe):
            pe.wait_ge(S["consts_in"], CONSTS)
            pe.transpose(bank[0][:, NB:NB + MEM], wsm[0:MEM, 0:D], ident[0:MEM, 0:MEM])
            pe.transpose(bank[0][:, NB + MEM:NB + 2 * MEM], wsm[0:MEM, D:2 * D], ident[0:MEM, 0:MEM])
            pe.transpose(bank[0][0:MEM, P:P + D], wsm[:, 3 * D:3 * D + MEM], ident)
            pe.transpose(bank[1][:, 0:NE * FB], b1S, ident[0:NE * FB, 0:NE * FB])
            pe.transpose(bank[1][:, NE * FB:NE * (FB + 1)], b2S, ident[0:NE, 0:NE]).then_inc(S["b_ps"], 1)
            pe.wait_ge(S["silu_ready"], 1)
            pe.transpose(bank[0][:, 0:NB], cS[:, 2, :], ident[0:NB, 0:NB]).then_inc(S["transposed"], 1)
            pe.wait_ge(S["copied"], 3)
            pe.wait_ge(S["wmod_in"], 16)
            pe.matmul(bank[2][:, 0:D], wsm[0:MEM, 2 * D:3 * D], woT[:], start=True, stop=True)
            pe.matmul(bank[3][0:MEM, 0:D], M0S[:], woT[:], start=True, stop=True)
            pe.matmul(bank[4][:, 0:3 * D], scT[:], wmS[:, 0:3 * D], start=True, stop=True)
            pe.matmul(bank[5][:, 0:3 * D], scT[:], wmS[:, 3 * D:6 * D], start=True, stop=True).then_inc(
                S["products"], 1)
            pe.wait_ge(S["setup_done"], 1)

            def transposes(n):
                pe.wait_ge(S["h_ready"], n + 1)
                at_least(pe, S["hT_ready"], n)
                for j in range(BC):
                    ins = pe.transpose(bank[0][:, j * P:(j + 1) * P], hn[:, n % 2, j, :], ident)
                ins.then_inc(S["hT_ps"], 1)

            def transposes2(n):
                pe.wait_ge(S["h2_ready"], n + 1)
                at_least(pe, S["h2T_ready"], n)
                for j in range(BC):
                    ins = pe.transpose(bank[5][:, j * P:(j + 1) * P], rows[:, n % RB, 0, j, 0:D], ident)
                ins.then_inc(S["h2T_ps"], 1)

            def keep_clock(times):
                for _ in range(times):
                    pe.matmul(bank[5][:].rearrange("p (c t) -> p c t", c=BC), ones[:],
                              ones[:].rearrange("p (a t) -> p a t", a=1).broadcast_to((P, BC, P)), start=True, stop=True)

            def projections(n):
                at_least(pe, S["h2T_ready"], n - 2)
                keep_clock(1)
                pe.wait_ge(S["hT_ready"], n + 1)
                at_least(pe, S["q_ready"], n)
                at_least(pe, S["k_ready"], n)
                at_least(pe, S["m_ready"], n * BC)
                pe.matmul(bank[1][0:2 * MEM, :], wqkv[:, 0:2 * MEM], hT[:], start=True, stop=True).then_inc(
                    S["qk_ps"], 1)

            def projections2(n):
                at_least(pe, S["v_ready"], n * 2)
                for j in range(BC):
                    ins = pe.matmul(kv[:, j // 2, j % 2 * (MEM + D):(j % 2 + 1) * (MEM + D)],
                                    hT[:, j * P:(j + 1) * P], wqkv[:, MEM:], start=True, stop=True)
                ins.then_inc(S["v_ps"], 1)

            def logits(n):
                pe.wait_ge(S["h2T_ready"], n + 1)
                at_least(pe, S["pos_ready"], n)
                for j in range(BC):
                    ins = pe.matmul(bank[6][:, j * NE:(j + 1) * NE], h2T[:, j * P:(j + 1) * P], WgS[:],
                                    start=True, stop=True)
                ins.then_inc(S["lg_ps"], 1)

            def middle(n):
                b = n % 2
                pe.wait_ge(S["q_ready"], n + 1)
                pe.wait_ge(S["k_ready"], n + 1)
                at_least(pe, S["a_ready"], n)
                for j in range(BC):
                    cols = slice(j * P, (j + 1) * P)
                    ins = pe.matmul(bank[4][:, cols], kT[:, b, cols], qT[:, b, cols], start=True, stop=True)
                ins.then_inc(S["s_ps"], 1)
                pe.wait_ge(S["v_ready"], n * 2 + 2)
                for j in range(BC):
                    ins = pe.matmul(bank[1][0:MEM, j * D:(j + 1) * D], kS[:, b, j, :], vS[:, b, j, :],
                                    start=True, stop=True)
                ins.then_inc(S["u_ps"], 1)

            def outputs(n):
                b = n % 2
                pe.wait_ge(S["a_ready"], n + 1)
                at_least(pe, S["o_read"], n)
                pe.wait_ge(S["m_ready"], n * BC + BC - 1)
                for j in range(BC):
                    cols = slice(j * P, (j + 1) * P)
                    pe.matmul(bank[7][:, cols], aS[:, j, :], vS[:, b, j, :], start=True, stop=False)
                    ins = pe.matmul(bank[7][:, cols], qT[:, b, cols], Mst[:, b, j, :], start=False, stop=True)
                ins.then_inc(S["o_ps"], 1)
                at_least(pe, S["h2T_ready"], n - 1)
                keep_clock(0)

            def ranks(n):
                pe.wait_ge(S["t_ready"], n + 1)
                at_least(pe, S["cum_ready"], n)
                r = bank[6][:, P:P + BC * NE].rearrange("p (c e) -> p c e", c=BC)
                pe.matmul(r, ones[:], cumb[:].rearrange("p (a e) -> p a e", a=1).broadcast_to((P, BC, NE)),
                          start=True, stop=False)
                for j in range(BC - 1):
                    pe.matmul(r[:, j + 1:, :], ones[:], T[:, j:j + 1, :].broadcast_to((P, BC - 1 - j, NE)),
                              start=False, stop=False)
                pe.matmul(r, tri[:], T[:], start=False, stop=True).then_inc(S["rk_ps"], 1)

            for n in range(NG + 2):
                if has(n - 1):
                    outputs(n - 1)
                if has(n):
                    transposes(n)
                    projections(n)
                if has(n - 2):
                    transposes2(n - 2)
                if has(n):
                    projections2(n)
                if has(n - 2):
                    logits(n - 2)
                if has(n):
                    middle(n)
                    at_least(pe, S["h2T_ready"], n - 1)
                    keep_clock(3)
                if has(n - 2):
                    ranks(n - 2)

            pe.wait_ge(S["cum_ready"], NG)
            pe.matmul(bank[6][:, 2 * P:2 * P + NE], ones[:], cumb[:], start=True, stop=True).then_inc(S["cnt_ps"], 1)
            pe.wait_ge(S["tab_cols"], 1)
            for i in range(2):
                ins = pe.matmul(bank[0][0:1, i * P:i * P + NTILE], tab[:, i:i + 1], ident[:, 0:NTILE],
                                start=True, stop=True)
            ins.then_inc(S["tab_ps"], 1)
            pe.wait_ge(S["table_ready"], 2)
            pe.wait_ge(S["split_lo"], 4)

            def tile(n):
                j, b = n, n.place % 2
                if j.exists(NTILE):
                    pe.wait_ge(tile_in[j.place], (j.turn + 1) * 16)
                    at_least(pe, S["th_ready"], j.n * 2 - 2)
                    for h in range(2):
                        ins = pe.transpose(bank[b][:, h * P:(h + 1) * P], tin[:, j.place, h, 0:D], ident)
                    ins.then_inc(S["th_ps"], 1)
                j = n.back(1)
                b = j.place % 2
                if j.exists(NTILE):
                    pe.wait_ge(S["w1_copied"], j.n * 2 + 2)
                    pe.wait_ge(S["th_ready"], j.n * 2 + 2)
                    at_least(pe, S["gelu"], FB * (j.n - 1))
                    for f in range(FB):
                        hid = bank[2 + 2 * b + f // 2][:, f % 2 * TR:(f % 2 + 1) * TR]
                        w1h, w1l = (W1s[:, b, i, f * P:(f + 1) * P] for i in range(2))
                        pe.matmul(hid, w1h, th[:, b, :], start=True, stop=False)
                        pe.matmul(hid, w1h, tl[:, b, :], start=False, stop=False)
                        pe.matmul(hid, w1l, th[:, b, :], start=False, stop=True).then_inc(S["mm1"], 1)
                j = n.back(2)
                b = j.place % 2
                if j.exists(NTILE):
                    y = bank[6 + b][:, 0:TR]
                    pe.wait_ge(S["w2_copied"], j.n + 1)
                    pe.wait_ge(S["gh_ready"], j.n + 1)
                    at_least(pe, S["y_ready"], j.n - 1)
                    for f in range(FB):
                        for i in range(2):
                            pe.matmul(y, W2s[:, b, f, i * D:(i + 1) * D], gh[:, b, f * TR:(f + 1) * TR],
                                      start=(f == 0 and i == 0), stop=False)
                    pe.wait_ge(S["gl_ready"], j.n + 1)
                    for f in range(FB):
                        ins = pe.matmul(y, W2s[:, b, f, 0:D], gl[:, b, f * TR:(f + 1) * TR],
                                        start=False, stop=(f == FB - 1))
                    ins.then_inc(S["y_ps"], 1)
                j = n.back(3)
                b = j.place % 2
                if j.exists(NTILE):
                    pe.wait_ge(S["yT_ready"], j.n + 1)
                    for h in range(2):
                        ins = pe.transpose(bank[6 + b][:, TR + h * P:TR + (h + 1) * P],
                                           yT[:, b, h * P:(h + 1) * P], ident)
                    ins.then_inc(S["yt_ps"], 1)
            straight(NTILE + 3, SLOTS, tile)


_INS = ["L0_attn_x", "L0_attn_Wq", "L0_attn_Wk", "L0_attn_Wv", "L0_attn_Wo", "L0_attn_gate", "L0_attn_M0",
        "L0_ffn_Wg", "L0_ffn_bg", "L0_ffn_W1", "L0_ffn_b1", "L0_ffn_W2", "L0_ffn_b2", "L0_c", "L0_wmod"]


def kernel(**inputs):
    import concourse.bacc as bacc
    from concourse.bass_utils import run_bass_kernel_spmd

    nc = bacc.Bacc("TRN2", target_bir_lowering=False, num_devices=1)
    arrays = {f"in_{name}": np.ascontiguousarray(inputs[name]) for name in _INS}
    arrays.update(shape_constants())
    args = [nc.dram_tensor(name, a.shape, mybir.dt.from_np(a.dtype), kind="ExternalInput").ap()
            for name, a in arrays.items()]
    out = nc.dram_tensor("out_0", (NB, NT, D), F32, kind="ExternalOutput").ap()
    routed = nc.dram_tensor("routed", (NROWS, ROWW), F32, kind="Internal").ap()
    y_rows = nc.dram_tensor("y_rows", (2 * NTOK, D), F32, kind="Internal").ap()
    build(nc, *args, out, routed, y_rows)
    return run_bass_kernel_spmd(nc, [arrays], core_ids=[0]).results[0]["out_0"]
```
